# Optimizing a Trainium2 kernel written in Bass

```python
import numpy as np
import jax
import jax.numpy as jnp

def _softmax(x, axis=-1):
    return jax.nn.softmax(x, axis=axis)

def _gelu(x):
    return jax.nn.gelu(x, approximate=True)

def _silu(x):
    return jax.nn.silu(x)

def _sigmoid(x):
    return jax.nn.sigmoid(x)

def _layernorm(x, axis=-1, eps=1e-05):
    m = jnp.mean(x, axis=axis, keepdims=True)
    v = jnp.var(x, axis=axis, keepdims=True)
    return (x - m) / jnp.sqrt(v + eps)

def _scatter_add(tgt, idx, src, axis=0):
    return tgt.at[idx].add(src)

def _segment_sum(src, seg, n):
    return jax.ops.segment_sum(src, seg, n)
kernel_name = 'mk_adaln_ffn_d2_seqx_r4_ee9ca3'

def setup_inputs(seed: int=0):
    np.random.seed(seed)
    _w = jnp.asarray

    def _rec_inputs():
        import jax
        import jax.numpy as jnp
        _rk = jax.random.key(seed)
        x = -7.109e-05 + 0.9999 * jax.random.normal(jax.random.fold_in(_rk, 1), (8, 256, 1024), jnp.float32)
        _lenS = 256 - jax.random.randint(jax.random.fold_in(_rk, 7), (8,), 0, max(1, 256 // 4) + 1, jnp.int32)
        _lenS2 = 256 - jax.random.randint(jax.random.fold_in(_rk, 8), (8,), 0, max(1, 256 // 4) + 1, jnp.int32)
        condB_thresholds = jax.random.uniform(jax.random.fold_in(_rk, 11), (8,), jnp.float32, 0.0, 1.82799)
        condB_deltas = jax.random.uniform(jax.random.fold_in(_rk, 12), (8,), jnp.float32, 0.0, 0.0232459)
        condB_zeropoints = jax.random.uniform(jax.random.fold_in(_rk, 13), (8,), jnp.float32, 0.0, 243)
        itok_B_1_7 = jax.random.randint(jax.random.fold_in(_rk, 14), (8,), 1, 8, jnp.int32)
        return (x, condB_thresholds, condB_deltas, condB_zeropoints, itok_B_1_7)
    x, condB_thresholds, condB_deltas, condB_zeropoints, itok_B_1_7 = _rec_inputs()

    def _L0_cond_setup():
        import jax, jax.numpy as jnp
        import numpy as np
        N_LEVELS = 64
        key = jax.random.key(seed)
        k1, k2, k3, k4 = jax.random.split(key, 4)
        x = jax.random.normal(k1, (4, 1024, 1024), dtype=jnp.float32)
        G = 4
        thresholds = jnp.sort(jax.random.uniform(k2, (G,), minval=0.2, maxval=3.0))[::-1].astype(jnp.float32)
        deltas = (jax.random.uniform(k3, (G,)) * 0.02 + 0.005).astype(jnp.float32)
        zero_points = jnp.round(jax.random.uniform(k4, (G,)) * (N_LEVELS - 1)).astype(jnp.float32)
        return {'x': x, 'thresholds': thresholds, 'deltas': deltas, 'zero_points': zero_points}
    _L0_cond_all = _L0_cond_setup()
    _L0_cond_in = {k: v for k, v in _L0_cond_all.items() if k in ()}
    del _L0_cond_all

    def _L0_ffn_setup():
        import jax, jax.numpy as jnp
        import numpy as np
        TOP_K = 2
        key = jax.random.key(seed)
        k1, k2, k3 = jax.random.split(key, 3)
        B, S, H, O, E = (2048, 1, 1024, 1024, 8)
        x = jax.random.normal(k1, (B, S, H), dtype=jnp.float32)
        gate_w = jax.random.normal(k2, (H, E), dtype=jnp.float32) * 0.02
        expert_w = jax.random.normal(k3, (E, H, O), dtype=jnp.float32) * 0.02
        return {'x': x, 'gate_w': gate_w, 'expert_w': expert_w}
    _L0_ffn_all = _L0_ffn_setup()
    _L0_ffn_in = {k: v for k, v in _L0_ffn_all.items() if k in ('gate_w', 'expert_w')}
    del _L0_ffn_all

    def _L1_cond_setup():
        import jax, jax.numpy as jnp
        import numpy as np
        B, S, D_IN, D_OUT = (4, 512, 1024, 1024)
        N_ADAPTERS, MAX_RANK = (8, 16)
        key = jax.random.key(seed)
        ks = jax.random.split(key, 7)
        x = jax.random.normal(ks[0], (B, S, D_IN), dtype=jnp.float32)
        weight = jax.random.normal(ks[1], (D_OUT, D_IN), dtype=jnp.float32) * (1.0 / np.sqrt(D_IN))
        bias = jax.random.normal(ks[2], (D_OUT,), dtype=jnp.float32) * 0.01
        lora_a_weights = jax.random.normal(ks[3], (N_ADAPTERS, MAX_RANK, D_IN), dtype=jnp.float32) * (1.0 / np.sqrt(D_IN))
        lora_b_weights = jax.random.normal(ks[4], (N_ADAPTERS, D_OUT, MAX_RANK), dtype=jnp.float32) * 0.02
        scaling_factors = jax.random.uniform(ks[5], (N_ADAPTERS,), dtype=jnp.float32, minval=0.5, maxval=2.0)
        adapter_id = jax.random.randint(ks[6], (B,), 0, N_ADAPTERS, dtype=jnp.int64)
        return {'x': x, 'weight': weight, 'bias': bias, 'lora_a_weights': lora_a_weights, 'lora_b_weights': lora_b_weights, 'scaling_factors': scaling_factors, 'adapter_id': adapter_id}
    _L1_cond_all = _L1_cond_setup()
    _L1_cond_in = {k: v for k, v in _L1_cond_all.items() if k in ('weight', 'bias', 'lora_a_weights', 'lora_b_weights', 'scaling_factors')}
    del _L1_cond_all

    def _L1_ffn_setup():
        import jax, jax.numpy as jnp
        import numpy as np
        IN_F = 1024
        OUT_F = 1024
        N_CLUSTERS = 64
        THRESHOLD = 0.01
        TEMPERATURE = 0.1
        BATCH, SEQ = (4, 512)
        key = jax.random.key(seed)
        k1, k2, k3, k4, k5 = jax.random.split(key, 5)
        s = 1.0 / np.sqrt(IN_F)
        return {'input': jax.random.normal(k1, (BATCH, SEQ, IN_F), dtype=jnp.float32), 'weight': jax.random.normal(k2, (OUT_F, IN_F), dtype=jnp.float32) * s, 'bias': jax.random.uniform(k3, (OUT_F,), dtype=jnp.float32, minval=-s, maxval=s), 'centroids': jax.random.normal(k4, (N_CLUSTERS, IN_F), dtype=jnp.float32) * s, 'assignments': jax.random.randint(k5, (OUT_F,), 0, N_CLUSTERS, dtype=jnp.int32)}
    _L1_ffn_all = _L1_ffn_setup()
    _L1_ffn_in = {k: v for k, v in _L1_ffn_all.items() if k in ('weight', 'bias', 'centroids', 'assignments')}
    del _L1_ffn_all
    return {'x': x, 'condB_thresholds': condB_thresholds, 'condB_deltas': condB_deltas, 'condB_zeropoints': condB_zeropoints, 'itok_B_1_7': itok_B_1_7, 'L0_ffn_gate_w': _L0_ffn_in['gate_w'], 'L0_ffn_expert_w': _L0_ffn_in['expert_w'], 'L1_cond_weight': _L1_cond_in['weight'], 'L1_cond_bias': _L1_cond_in['bias'], 'L1_cond_lora_a_weights': _L1_cond_in['lora_a_weights'], 'L1_cond_lora_b_weights': _L1_cond_in['lora_b_weights'], 'L1_cond_scaling_factors': _L1_cond_in['scaling_factors'], 'L1_ffn_weight': _L1_ffn_in['weight'], 'L1_ffn_bias': _L1_ffn_in['bias'], 'L1_ffn_centroids': _L1_ffn_in['centroids'], 'L1_ffn_assignments': _L1_ffn_in['assignments']}

def reference(x, condB_thresholds, condB_deltas, condB_zeropoints, itok_B_1_7, L0_ffn_gate_w, L0_ffn_expert_w, L1_cond_weight, L1_cond_bias, L1_cond_lora_a_weights, L1_cond_lora_b_weights, L1_cond_scaling_factors, L1_ffn_weight, L1_ffn_bias, L1_ffn_centroids, L1_ffn_assignments):
    import jax
    import jax.numpy as jnp

    def _L0_cond_ref(x, thresholds, deltas, zero_points):
        import jax, jax.numpy as jnp
        import numpy as np
        N_LEVELS = 64
        G = thresholds.shape[0]
        gi = jnp.sum(jnp.abs(x)[..., None] <= thresholds, axis=-1)
        idx = jnp.minimum(gi, G - 1)
        d = deltas[idx]
        zp = zero_points[idx]
        x_quant = jnp.clip(jnp.round(x / d) + zp, 0, N_LEVELS - 1)
        x_dequant = (x_quant - zp) * d
        return jnp.where(gi == G, jnp.float32(0), x_dequant)

    def _L0_ffn_ref(x, gate_w, expert_w):
        import jax, jax.numpy as jnp
        import numpy as np
        TOP_K = 2
        E = gate_w.shape[-1]
        logits = jnp.einsum('bsh,he->bse', x, gate_w)
        topv, topi = jax.lax.top_k(logits, TOP_K)
        w = jax.nn.softmax(topv, axis=-1)
        onehot = jax.nn.one_hot(topi, E, dtype=x.dtype)
        w_e = jnp.einsum('bske,bsk->bse', onehot, w)
        out = jnp.einsum('bsh,eho,bse->bso', x, expert_w, w_e)
        return out

    def _L1_cond_ref(x, weight, bias, lora_a_weights, lora_b_weights, scaling_factors, adapter_id):
        import jax, jax.numpy as jnp
        import numpy as np
        B, S, D_IN, D_OUT = (4, 512, 1024, 1024)
        N_ADAPTERS, MAX_RANK = (8, 16)
        base = jnp.einsum('bsi,oi->bso', x, weight) + bias
        a_sel = lora_a_weights[adapter_id]
        b_sel = lora_b_weights[adapter_id]
        scale = scaling_factors[adapter_id]
        low = jnp.einsum('bsi,bri->bsr', x, a_sel)
        delta = jnp.einsum('bsr,bor->bso', low, b_sel)
        return base + scale[:, None, None] * delta

    def _L1_ffn_ref(input, weight, bias, centroids, assignments):
        import jax, jax.numpy as jnp
        import numpy as np
        IN_F = 1024
        OUT_F = 1024
        N_CLUSTERS = 64
        THRESHOLD = 0.01
        TEMPERATURE = 0.1
        BATCH, SEQ = (4, 512)
        shape = input.shape
        x = input.reshape(-1, shape[-1])
        dots = jax.nn.softmax(x @ centroids.T / TEMPERATURE, axis=-1)
        hits = dots > THRESHOLD
        query_sel = jnp.any(hits, axis=1)
        cluster_sel = jnp.any(hits, axis=0)
        row_sel = cluster_sel[assignments]
        dense = x @ weight.T + bias
        out = jnp.where(query_sel[:, None] & row_sel[None, :], dense, jnp.zeros((), dense.dtype))
        return out.reshape(*shape[:-1], -1)
    x = x + _L0_ffn_ref(_L0_cond_ref(x, condB_thresholds, condB_deltas, condB_zeropoints), L0_ffn_gate_w, L0_ffn_expert_w)
    x = x + _L1_ffn_ref(_L1_cond_ref(x, L1_cond_weight, L1_cond_bias, L1_cond_lora_a_weights, L1_cond_lora_b_weights, L1_cond_scaling_factors, itok_B_1_7), L1_ffn_weight, L1_ffn_bias, L1_ffn_centroids, L1_ffn_assignments)
    return x

_drawn_inputs = setup_inputs


def setup_inputs(seed=0):
    import zlib

    import numpy as np

    out = dict(_drawn_inputs(seed))
    spreads = {}
    factors = {'L1_cond_bias': 8.0, 'L1_cond_scaling_factors': 3.353, 'L1_ffn_bias': 5.805}
    for name, (base, spread) in spreads.items():
        noise = np.random.default_rng([zlib.crc32(name.encode()), seed]).standard_normal(out[name].shape)
        drawn = base * np.exp(spread * noise) if base else spread * noise
        out[name] = jnp.asarray(drawn.astype(out[name].dtype))
    for name, factor in factors.items():
        out[name] = (out[name] * factor).astype(out[name].dtype)
    return out
```

```python
from contextlib import ExitStack

import numpy as np

import concourse.bass as bass
from concourse import mybir

F32 = mybir.dt.float32
F32R = mybir.dt.float32r
BF16 = mybir.dt.bfloat16
I32 = mybir.dt.int32
U32 = mybir.dt.uint32
U8 = mybir.dt.uint8
ALU = mybir.AluOpType
ACT = mybir.ActivationFunctionType
AX = mybir.AxisListType

P = 128
H = 1024
KC = H // P
TOK = 2048
NT = TOK // P
E = 8
TOPK = 2
G = 8
LEVELS = 64
CL = 64
HX = H + CL
R = 16
A = 8
MT = TOK * TOPK // P + E - 1
NB = 512
W2X = KC * HX
WE = KC * H
SLOT1 = 2 * W2X
ROUND = 1.5 * 2.0 ** 23
TEMPERATURE = 0.1
THRESHOLD = 0.01


class Chain:

    def __init__(self, engine, sem):
        self.engine, self.sem, self.base, self.n = engine, sem, 0, 0

    def __call__(self, instruction):
        self.n += 1
        instruction.then_inc(self.sem, 1)
        self.engine.wait_ge(self.sem, self.base + self.n)

    def turn(self, i, first, per):
        self.base, self.n = first + i * per, 0

    def here(self):
        return self.base + self.n


def build(nc, x, thresholds, deltas, zero_points, adapter, gate_w, expert_w, w1, b1, lora_a, lora_b,
          scaling, w2, b2, centroids, assignments, out):
    def scratch(name, shape, dt):
        return nc.dram_tensor(name, shape, dt).ap()

    q_dram = scratch("q_dram", [TOK, H], F32)
    xs_dram = scratch("xs_dram", [MT * P, H], F32)
    y_dram = scratch("y_dram", [MT * P, H], F32)
    m_dram = scratch("m_dram", [2, P, KC, HX], F32)
    x1_dram = scratch("x1_dram", [TOK, H], F32)

    with ExitStack() as ctx:
        def sb(name, shape, dt=F32):
            return ctx.enter_context(nc.sbuf_tensor(name, shape, dt))

        def sem(name):
            return ctx.enter_context(nc.semaphore(name))

        with ExitStack() as under:
            def over(name, shape, dt=F32):
                return under.enter_context(nc.sbuf_tensor(name, shape, dt))
            over("under_slot0", [P, SLOT1])
            mev = over("mev", [P, 2, HX], F32R)
            qrow = over("qrow", [P, 2, H])
            qT = over("qT", [P, KC, P])
            rbuf = over("rbuf", [P, 10, NT, E])
            mt_cmp = over("mt_cmp", [P, MT, E - 1])
            with ExitStack() as inner:
                def first(name, shape, dt=F32):
                    return inner.enter_context(nc.sbuf_tensor(name, shape, dt))
                xa = first("xa", [P, 2, H])
                inv_sel = first("inv_sel", [P, H])
                low_sel = first("low_sel", [P, H])
                del_sel = first("del_sel", [P, H])
                steps = first("steps", [P, H])
                mask = first("mask", [P, H], U8)
            hotB = over("hotB", [P, 2 * NT, P], BF16)
            hotA = over("hotA", [P, 2 * NT, MT], BF16)
            hotX = over("hotX", [P, 2 * NT, 2 * MT], BF16)
        with ExitStack() as under:
            under.enter_context(nc.sbuf_tensor("under_slot0b", [P, SLOT1], F32))
            dense = under.enter_context(nc.sbuf_tensor("dense", [P, NT, H], F32))
        wslots = sb("wslots", [P, 2 * W2X + 2 * WE], F32R)
        ath = sb("ath", [P, 2, KC, P], F32R)
        bwx = sb("bwx", [P, 2, HX], F32R)
        split = sb("split", [P, 2, 2, KC, P], F32R)
        stage = sb("stage", [P, 4, H])
        gring = sb("gring", [P, 2, H])
        tin = sb("tin", [P, 2, H])
        yout = sb("yout", [P, 2, H])
        biasx = sb("biasx", [P, HX])
        pickT = sb("pickT", [CL, H], BF16)
        ident = sb("ident", [P, P])
        rowi = sb("rowi", [P, P])
        parti = sb("parti", [P, 1])
        tri = sb("tri", [P, P], BF16)
        ones = sb("ones", [P, P], BF16)
        gw = sb("gw", [P, KC, E])
        b1c = sb("b1c", [P, KC])
        par = sb("par", [P, 4, G])
        par2 = sb("par2", [P, 3, G])
        edge = sb("edge", [P, 2])
        adp = sb("adp", [P, E], I32)
        adpf = sb("adpf", [P, E])
        comb = sb("comb", [P, E])
        sc = sb("sc", [P, 8, E])
        rcol = sb("rcol", [P, 8, NT])
        wts = sb("wts", [P, 2, NT])
        slots = sb("slots", [P, 2, NT])
        sli = sb("sli", [P, 2, NT], I32)
        sli2 = sb("sli2", [P, 2, 2, NT], I32)
        idx = sb("idx", [P, 2, 2], U32)
        slotu = sb("slotu", [P, 2, NT], U32)
        slo = sb("slo", [P, 2, NT])
        shi = sb("shi", [P, 2, NT])
        tcol = sb("tcol", [P, 2, NT])
        mt_row = sb("mt_row", [P, MT])
        mt_exp = sb("mt_exp", [P, MT])
        mt_int = sb("mt_int", [P, MT], I32)
        mt_par = sb("mt_par", [P, MT], I32)
        mt_need = sb("mt_need", [P, MT], I32)
        mt_need1 = sb("mt_need1", [P, MT], I32)
        freeat = sb("freeat", [P, E + 1], I32)
        tint = sb("tint", [P, E], I32)
        toku = sb("toku", [P, MT], U32)
        lows = sb("lows", [P, P])
        lowr = sb("lowr", [P, 2, P], F32R)
        zl = sb("zl", [P, CL])
        el = sb("el", [P, CL])
        hits = sb("hits", [P, CL])
        cacc = sb("cacc", [P, CL])
        caccb = sb("caccb", [P, CL], BF16)
        smx = sb("smx", [P, 4])
        qsel = sb("qsel", [P, NT])
        cselb = sb("cselb", [CL, P], BF16)
        clu = sb("clu", [CL, 1])

        wf = wslots[:, :].bitcast(F32)
        splitf = split[:, :, :, :, :].bitcast(F32)
        athf = ath[:, :, :, :].bitcast(F32)
        bwxf = bwx[:, :, :].bitcast(F32)
        mevf = mev[:, :, :].bitcast(F32)
        lowrf = lowr[:, :, :].bitcast(F32)

        def w2part(tensor, part):
            return tensor[:, part * W2X:(part + 1) * W2X].rearrange("p (k n) -> p k n", k=KC)

        def expart(tensor, odd, part):
            o = odd * SLOT1 + part * WE
            return tensor[:, o:o + WE].rearrange("p (k n) -> p k n", k=KC)

        main = ctx.enter_context(nc.psum_tensor("main", [P, 2, H], F32))
        pst = ctx.enter_context(nc.psum_tensor("pst", [P, KC, P], F32))
        psg = ctx.enter_context(nc.psum_tensor("psg", [P, NB], F32))
        psl = ctx.enter_context(nc.psum_tensor("psl", [P, NB], F32))

        const_in = sem("const_in")
        iota_done = sem("iota_done")
        consts = sem("consts")
        lora_in = sem("lora_in")
        stage_in = [sem(f"stage_in{i}") for i in range(4)]
        w1_in = [sem(f"w1_in{i}") for i in range(2)]
        setup_T = sem("setup_T")
        setup_hi = sem("setup_hi")
        setup_lo = sem("setup_lo")
        split_hi = sem("split_hi")
        split_lo = sem("split_lo")
        prod = sem("prod")
        prod_hi = sem("prod_hi")
        prod_lo = sem("prod_lo")
        m_free = sem("m_free")
        m_store = sem("m_store")
        x_in = [sem(f"x_in{i}") for i in range(2)]
        q_ready = sem("q_ready")
        q_store = [sem(f"q_store{i}") for i in range(2)]
        q_free = sem("q_free")
        x_used = sem("x_used")
        q_T = sem("q_T")
        q_Tout = sem("q_Tout")
        gate = sem("gate")
        gate_out = sem("gate_out")
        dve_chain = sem("dve_chain")
        exp_in = sem("exp_in")
        exp_out = sem("exp_out")
        hots_ready = sem("hots_ready")
        counted = sem("counted")
        slots_ready = sem("slots_ready")
        placed = sem("placed")
        routed = sem("routed")
        idx_ready = sem("idx_ready")
        idx_seen = sem("idx_seen")
        mask_seen = sem("mask_seen")
        g_in = [sem(f"g_in{i}") for i in range(2)]
        xs_store = [sem(f"xs_store{i}") for i in range(2)]
        wch_hi = sem("wch_hi")
        wch_lo = sem("wch_lo")
        one_lo = sem("one_lo")
        tin_in = [sem(f"tin_in{i}") for i in range(2)]
        t_T = sem("t_T")
        t_split = sem("t_split")
        tile_done = sem("tile_done")
        y_out = sem("y_out")
        y_store = [sem(f"y_store{i}") for i in range(2)]
        m_in = sem("m_in")
        xc_in = [sem(f"xc_in{i}") for i in range(2)]
        ga_in = [sem(f"ga_in{i}") for i in range(2)]
        gb_in = [sem(f"gb_in{i}") for i in range(2)]
        x1_ready = sem("x1_ready")
        x1_store = [sem(f"x1_store{i}") for i in range(2)]
        x1_T = sem("x1_T")
        x1_hi = sem("x1_hi")
        x1_lo = sem("x1_lo")
        low_done = sem("low_done")
        low_scaled = sem("low_scaled")
        low_hi = sem("low_hi")
        low_lo = sem("low_lo")
        layer_done = sem("layer_done")
        dense_out = sem("dense_out")
        scores_out = sem("scores_out")
        nb_ready = sem("nb_ready")
        soft_done = sem("soft_done")
        cacc_ready = sem("cacc_ready")
        clu_done = sem("clu_done")
        csel_ready = sem("csel_ready")
        rowsel_done = sem("rowsel_done")
        xr_in = [sem(f"xr_in{i}") for i in range(4)]
        fin_ready = sem("fin_ready")
        out_store = [sem(f"out_store{i}") for i in range(2)]

        N_CONST = 9
        block = ctx.enter_context(nc.Block())

        def rows(i):
            return slice(i * P, (i + 1) * P) if isinstance(i, int) else bass.ds(i * P, P)

        w1_v = w1.rearrange("(k p) (j i) -> j p k i", p=P, i=P)
        ew_v = expert_w.rearrange("e (k p) n -> (e k) p n", p=P)

        @block.sync
        def _(sp):
            sp.dma_start(stage[0:CL, 0, :], centroids).then_inc(stage_in[0], 16)
            sp.dma_start(stage[:, 1, :], lora_a.rearrange("a r i -> (a r) i")).then_inc(stage_in[1], 16)
            for n, source in enumerate((thresholds, deltas, zero_points, scaling)):
                sp.dma_start(par[:, n, :], source.partition_broadcast(P)).then_inc(const_in, 16)
            sp.dma_start(adp[:, :], adapter.partition_broadcast(P)).then_inc(const_in, 16)
            sp.dma_start(gw[:, :, :], gate_w.rearrange("(k p) e -> p k e", p=P)).then_inc(const_in, 16)
            with nc.allow_non_contiguous_dma(reason="a small column"):
                sp.dma_start(b1c[:, :], b1.rearrange("(k p) -> p k", p=P)).then_inc(const_in, 16)
            sp.dma_start(biasx[:, 0:H], b2.partition_broadcast(P)).then_inc(const_in, 16)
            sp.dma_start(gring[0:CL, 0, :].bitcast(I32),
                         assignments.partition_broadcast(CL)).then_inc(const_in, 16)
            for b in range(2):
                sp.dma_start(xa[:, b, :], x[rows(b), :]).then_inc(x_in[b], 16)
            with sp.Fori(0, KC // 2) as i:
                for b in range(2):
                    sp.wait_ge(setup_T, 2 * i + b + 1)
                    sp.dma_start(stage[:, b, :], w2[rows(2 * i + b), :]).then_inc(stage_in[b], 16)
            sp.wait_ge(setup_T, 2 + KC - 1)
            for k in range(KC):
                sp.dma_start(stage[:, 0, k * P:(k + 1) * P].rearrange("p (a r) -> p a r", a=A),
                             lora_b[:, k * P:(k + 1) * P, :].rearrange("a p r -> p a r")
                             ).then_inc(lora_in, 16)

            def quantised(i, more):
                for b in range(2):
                    sp.wait_ge(q_ready, 2 * i + b + 1)
                    sp.dma_start(q_dram[rows(2 * i + b), :], qrow[:, b, :]).then_inc(q_store[b], 16)
                    if more:
                        sp.dma_start(xa[:, b, :], x[rows(2 * i + b + 2), :]).then_inc(x_in[b], 16)

            with sp.Fori(0, NT // 2 - 1) as i:
                quantised(i, True)
            quantised(NT // 2 - 1, False)

            for b in range(2):
                sp.wait_ge(xs_store[b], 16)
                sp.dma_start(tin[:, b, :], xs_dram[rows(b), :]).then_inc(tin_in[b], 16)

            def turn(i, loads):
                for b in range(2):
                    if b in loads:
                        sp.wait_ge(xs_store[b], 16 * i + 32)
                        sp.wait_ge(t_T, 2 * i + b + 1)
                        sp.dma_start(tin[:, b, :], xs_dram[rows(2 * i + b + 2), :]).then_inc(tin_in[b], 16)
                    sp.wait_ge(y_out, 2 * i + b + 3)
                    sp.dma_start(y_dram[rows(2 * i + b), :], yout[:, b, :]).then_inc(y_store[b], 16)

            with sp.Fori(0, MT // 2 - 1) as i:
                turn(i, (0, 1))
            turn(MT // 2 - 1, (0,))
            sp.wait_ge(y_out, MT + 2)
            sp.dma_start(y_dram[rows(MT - 1), :], yout[:, 0, :]).then_inc(y_store[0], 16)

            sp.wait_ge(wch_lo, (E - 1) * KC)
            with sp.Fori(0, NT // 2) as i:
                for b in range(2):
                    sp.wait_ge(x1_ready, 2 * i + b + 1)
                    sp.dma_start(stage[:, b, :], x[rows(2 * i + b), :]).then_inc(xc_in[b], 16)
                    sp.wait_ge(x1_ready, 2 * i + b + 3)
                    sp.dma_start(x1_dram[rows(2 * i + b), :], yout[:, b, :]).then_inc(x1_store[b], 16)
            for b in range(2):
                sp.wait_ge(x1_store[b], 16 * NT // 2)

            for t in range(4):
                sp.dma_start(stage[:, t, :], x1_dram[rows(t), :]).then_inc(xr_in[t], 16)

            def result(i, more):
                for c in range(4):
                    sp.wait_ge(fin_ready, 4 * i + c + 1)
                    sp.dma_start(out[rows(4 * i + c), :], yout[:, c % 2, :]).then_inc(out_store[c % 2], 16)
                    if more:
                        sp.dma_start(stage[:, c, :], x1_dram[rows(4 * i + c + 4), :]).then_inc(xr_in[c], 16)

            with sp.Fori(0, NT // 4 - 1) as i:
                result(i, True)
            result(NT // 4 - 1, False)
            for b in range(2):
                sp.wait_ge(out_store[b], 16 * NT // 2)

        @block.gpsimd
        def _(pool):
            nc.gpsimd.memset(ident[:, :], 0.0).then_inc(iota_done, 1)
            pool.wait_ge(iota_done, 1)
            nc.gpsimd.affine_select(out=ident[:, :], in_=ident[:, :], compare_op=ALU.not_equal, fill=1.0,
                                    base=0, pattern=[[-1, P]], channel_multiplier=1).then_inc(iota_done, 1)
            kw = dict(allow_small_or_imprecise_dtypes=True)
            nc.gpsimd.iota(rowi[:, :], [[1, P]], base=0, channel_multiplier=0, **kw).then_inc(iota_done, 1)
            nc.gpsimd.iota(parti[:, :], [[0, 1]], base=0, channel_multiplier=1, **kw).then_inc(iota_done, 1)
            nc.gpsimd.iota(tcol[:, :, :], [[0, 2], [1, NT]], base=0, channel_multiplier=0,
                           **kw).then_inc(iota_done, 1)
            nc.gpsimd.iota(mt_row[:, :], [[1, MT]], base=0, channel_multiplier=0, **kw).then_inc(iota_done, 1)
            nc.gpsimd.memset(sc[:, 7, :], 1.0).then_inc(iota_done, 1)
            pool.wait_ge(iota_done, 7)
            nc.gpsimd.affine_select(out=sc[:, 7, :], in_=sc[:, 7, :], compare_op=ALU.is_ge, fill=0.0,
                                    base=0, pattern=[[-R, A]], channel_multiplier=1).then_inc(iota_done, 1)
            pool.wait_ge(iota_done, 8)
            nc.gpsimd.affine_select(out=sc[:, 7, :], in_=sc[:, 7, :], compare_op=ALU.is_ge, fill=0.0,
                                    base=R - 1, pattern=[[R, A]], channel_multiplier=-1).then_inc(iota_done, 1)
            nc.gpsimd.iota(sc[:, 6, :], [[-1, E]], base=E, channel_multiplier=0, **kw).then_inc(iota_done, 1)
            nc.gpsimd.iota(sc[:, 5, :], [[1, A]], base=0, channel_multiplier=0, **kw).then_inc(iota_done, 1)

            pool.sem_inc(m_free, 1)
            pool.wait_ge(setup_T, 2 + KC)

            def load(j, b):
                pool.wait_ge(split_lo, j + 1)
                pool.dma_start(stage[:, 1 - b, :].rearrange("p (k i) -> p k i", k=KC),
                               w1_v[j]).then_inc(w1_in[1 - b], 16)

            def store(j):
                pool.wait_ge(prod_lo, j + 3)
                pool.dma_start(m_dram[:, :, j, :].rearrange("h p n -> p h n"), mevf).then_inc(m_store, 16)
                pool.wait_ge(m_store, 16 * (j + 1))
                pool.sem_inc(m_free, 1)

            load(0, 0)
            for j in range(1, KC):
                load(j, j % 2)
                store(j - 1)
            store(KC - 1)

            def low_part(n, odd, c):
                pool.wait_ge(wch_hi, n + 1)
                nc.gpsimd.tensor_tensor(expart(wslots, odd, 1)[:, c, :], stage[:, c % 4, :],
                                        expart(wf, odd, 0)[:, c, :], ALU.subtract).then_inc(wch_lo, 1)

            for c in range(KC):
                low_part(c, 0, c)
            pool.wait_ge(routed, 1)
            for b in range(2):
                pool.wait_ge(q_store[b], 16 * NT // 2)

            def gather(source, table, column, n, to, b, landed):
                copies[0] += 1
                nc.gpsimd.tensor_copy(idx[:, n, b:b + 1], table[:, column]).then_inc(idx_ready, 1)
                pool.wait_ge(idx_ready, copies[1] + copies[0])
                pool.sem_inc(idx_seen, 1)
                nc.gpsimd.indirect_dma_start(
                    out=to[:, b, :], out_offset=None, in_=source,
                    in_offset=bass.IndirectOffsetOnAxis(ap=idx[:, n, b:b + 1], axis=0)).then_inc(landed[b], 16)

            def put(i, s, b):
                pool.wait_ge(g_in[b], 16 * i + 16)
                pool.dma_start(xs_dram[rows(s), :], gring[:, b, :]).then_inc(xs_store[b], 16)

            copies = [0, 0]
            for b in range(2):
                gather(q_dram, toku, slice(b, b + 1), 0, gring, b, g_in)

            def turn(i, gathers):
                for b in range(2):
                    put(i, 2 * i + b, b)
                    if b in gathers:
                        pool.wait_ge(xs_store[b], 16 * i + 16)
                        gather(q_dram, toku, bass.ds(2 * i + b + 2, 1), 0, gring, b, g_in)

            with pool.Fori(0, MT // 2 - 1) as i:
                copies[:] = [0, 2 + 2 * i]
                turn(i, (0, 1))
            copies[:] = [0, 2 + 2 * (MT // 2 - 1)]
            turn(MT // 2 - 1, (0,))
            put(MT // 2, MT - 1, 0)
            for b in range(2):
                pool.wait_ge(xs_store[b], 16 * (MT // 2 + 1 - b))
            with pool.Fori(1, E // 2) as pair:
                for odd in range(2):
                    for c in range(KC):
                        low_part(pair * 2 * KC + odd * KC + c, odd, c)

            pool.wait_ge(y_store[0], 16 * (MT // 2 + 1))
            pool.wait_ge(y_store[1], 16 * (MT // 2))
            pool.wait_ge(t_T, MT)
            with pool.Fori(0, NT // 2) as i:
                copies[:] = [0, MT + 4 * i]
                for b in range(2):
                    pool.wait_ge(x1_ready, 2 * i + b + 1)
                    for n, (to, landed) in enumerate(((gring, ga_in), (tin, gb_in))):
                        gather(y_dram, slotu[:, n, :], bass.ds(2 * i + b, 1), n, to, b, landed)

        @block.scalar
        def _(act):
            def setup_item(n, b, source_shape, to):
                act.wait_ge(setup_T, n + 1)
                nc.scalar.copy(to, source_shape).then_inc(setup_hi, 1)

            setup_item(0, 0, main[:, 0, 0:KC * CL].rearrange("p (k c) -> p k c", k=KC),
                       w2part(wslots, 0)[:, :, H:HX])
            setup_item(1, 1, main[:, 1, :].rearrange("p (k c) -> p k c", k=KC), ath[:, 0, :, :])
            with act.Fori(0, KC // 2) as i:
                for b in range(2):
                    setup_item(2 * i + b + 2, b, main[:, b, :].rearrange("p (k c) -> p k c", k=KC),
                               w2part(wslots, 0)[:, :, bass.ds(i * 2 * P + b * P, P)])
            act.wait_ge(const_in, 16 * N_CONST)
            act.wait_ge(lora_in, 16 * KC)
            nc.scalar.copy(split[:, 0, 0, :, :], stage[:, 0, :].rearrange("p (k i) -> p k i", k=KC)
                           ).then_inc(split_hi, 1)
            nc.scalar.copy(split[:, 1, 0, :, :], b1c[:, :].unsqueeze(2).broadcast_to((P, KC, P))
                           ).then_inc(split_hi, 1)
            act.wait_ge(prod, 1)
            nc.scalar.copy(bwx[:, 0, 0:H], main[:, 0, :]).then_inc(prod_hi, 1)
            nc.scalar.copy(bwx[:, 0, H:HX], psg[:, 0:CL]).then_inc(prod_hi, 1)
            act.sem_inc(gate_out, 1)
            act.sem_inc(q_free, 2)

            def tile(t, b, stored):
                act.wait_ge(q_T, t + 1)
                nc.scalar.copy(qT[:, :, :], pst[:, :, :]).then_inc(q_Tout, 1)
                act.wait_ge(gate, t + 1)
                nc.scalar.copy(rbuf[:, 0, bass.ds(t, 1), :],
                               psl[:, 0:E].unsqueeze(1)).then_inc(gate_out, 1)
                act.wait_ge(q_store[b], stored)
                act.sem_inc(q_free, 1)

            with act.Fori(0, KC // 2) as i:
                for b in range(2):
                    j = 2 * i + b
                    act.wait_ge(w1_in[1 - b], 16 * i + 16)
                    act.wait_ge(prod, j + 1)
                    nc.scalar.copy(split[:, b, 0, :, :],
                                   stage[:, 1 - b, :].rearrange("p (k i) -> p k i", k=KC)
                                   ).then_inc(split_hi, 1)
                    act.wait_ge(prod, j + 3)
                    act.wait_ge(m_free, j + 1)
                    nc.scalar.copy(mev[:, 0, 0:H], main[:, b, :]).then_inc(prod_hi, 1)
                    nc.scalar.copy(mev[:, 0, H:HX], psg[:, b * CL:(b + 1) * CL]).then_inc(prod_hi, 1)
                    for c in range(2):
                        tile(4 * i + 2 * b + c, c, 32 * i + 16 * b + 16)

            def fetch(n, c):
                act.dma_start(stage[:, c % 4, :], ew_v[n] if isinstance(n, int) else
                              ew_v[bass.ds(n, 1)].rearrange("o p n -> p (o n)")).then_inc(stage_in[c % 4], 16)

            before = (16 * (1 + KC // 2), 16 * (1 + KC // 2), 0, 0)

            def high_part(n, odd, c, last):
                act.wait_ge(stage_in[c % 4], before[c % 4] + 16 * (c // 4 + 1) + (n - c) * 4)
                nc.scalar.copy(expart(wslots, odd, 0)[:, c, :], stage[:, c % 4, :]).then_inc(wch_hi, 1)
                if not last:
                    if not isinstance(n, int) or n > 2 * KC:
                        act.wait_ge(wch_lo, n - KC)
                    elif n > KC:
                        act.wait_ge(one_lo, n - KC + 1)
                    elif n > 0:
                        act.wait_ge(wch_lo, n)
                    fetch(n + 3, (c + 3) % 4)

            act.wait_ge(split_lo, KC + 2)
            for c in range(3):
                fetch(c, c)
            act.wait_ge(prod, KC + 2)
            for c in range(KC):
                high_part(c, 0, c, False)
            act.wait_ge(exp_in, 1)
            nc.scalar.activation(rcol[:, 3, :], rcol[:, 2, :], ACT.Exp).then_inc(exp_out, 1)
            act.wait_ge(routed, 1)
            act.wait_ge(m_store, 16 * KC)
            for c in range(KC):
                high_part(KC + c, 1, c, False)

            def expert(e, odd, last):
                need = act.value_load(freeat[0:1, e:e + 1] if isinstance(e, int)
                                      else freeat[0:1, bass.ds(e, 1)], min_val=1, max_val=MT + 1)
                act.wait_ge(tile_done, need)
                for c in range(KC):
                    high_part(e * KC + c, odd, c, last and c + 3 >= KC)

            act.wait_ge(one_lo, KC + 1)
            with act.Fori(1, E // 2 - 1) as pair:
                for odd in range(2):
                    expert(pair * 2 + odd, odd, False)
            expert(E - 2, 0, False)
            expert(E - 1, 1, True)
            need = act.value_load(freeat[0:1, E:E + 1], min_val=1, max_val=MT + 1)
            act.wait_ge(tile_done, need)
            act.wait_ge(m_store, 16 * KC)
            for part in range(2):
                act.dma_start(w2part(wf, part), m_dram[part]).then_inc(m_in, 16)

            with act.Fori(0, NT // 2) as i:
                for b in range(2):
                    t = 2 * i + b
                    act.wait_ge(x1_T, t + 1)
                    nc.scalar.copy(split[:, b, 0, :, :], pst[:, :, :]).then_inc(x1_hi, 1)
                    act.wait_ge(low_scaled, t + 1)
                    nc.scalar.copy(lowr[:, 0, :], lows[:, :]).then_inc(low_hi, 1)
                    act.wait_ge(nb_ready, t + 1)
                    nc.scalar.activation(el[:, :], zl[:, :], ACT.Exp, bias=smx[:, 1:2], scale=1.0 / TEMPERATURE,
                                         accum_out=smx[:, 2:3]).then_inc(soft_done, 1)

        @block.vector
        def _(dve):
            V = nc.vector
            chain = Chain(dve, dve_chain)
            dve.sem_inc(tile_done, 1)
            dve.sem_inc(y_out, 2)
            dve.sem_inc(one_lo, 1)
            dve.sem_inc(x1_ready, 2)
            dve.sem_inc(dense_out, 2)
            dve.sem_inc(scores_out, 1)
            dve.wait_ge(const_in, 16 * N_CONST)
            dve.wait_ge(iota_done, 11)
            V.max(par2[:, 0, :], par[:, 0, :])
            V.reciprocal(par2[:, 1, :], par[:, 1, :])
            V.tensor_scalar(par2[:, 2, :], par[:, 2, :], -1.0, None, ALU.mult)
            V.memset(edge[:, 0:1], 0.0)
            V.memset(edge[:, 1:2], -1.0)
            V.memset(ones[:, :], 1.0)
            V.memset(cacc[:, :], 0.0)
            V.memset(freeat[:, 0:2], 1)
            V.tensor_scalar(tri[:, :], rowi[:, :], parti[:, :], None, ALU.is_gt)
            chain(V.tensor_copy(gring[0:CL, 1, :], gring[0:CL, 0, :].bitcast(I32)))
            V.tensor_scalar(pickT[:, :], gring[0:CL, 1, :], parti[0:CL, :], None, ALU.is_equal)
            chain(V.tensor_tensor(sc[:, 0, :], sc[:, 7, :], par[:, 3, :], ALU.mult))
            chain(V.tensor_reduce(sc[:, 1, 0:1], sc[:, 0, :], axis=AX.X, op=ALU.add))
            chain(V.tensor_tensor(sc[:, 2, :], sc[:, 7, :], sc[:, 5, :], ALU.mult))
            chain(V.tensor_reduce(sc[:, 1, 1:2], sc[:, 2, :], axis=AX.X, op=ALU.add))
            chain(V.tensor_copy(adpf[:, :], adp[:, :]))
            V.tensor_scalar(comb[:, :], adpf[:, :], sc[:, 1, 1:2], sc[:, 1, 0:1], ALU.is_equal,
                            ALU.mult).then_inc(consts, 1)

            def setup_item(n, source, hi, to):
                dve.wait_ge(setup_hi, n + 1)
                V.tensor_tensor(to, source, hi, ALU.subtract).then_inc(setup_lo, 1)

            setup_item(0, main[:, 0, 0:KC * CL].rearrange("p (k c) -> p k c", k=KC),
                       w2part(wf, 0)[:, :, H:HX], w2part(wslots, 1)[:, :, H:HX])
            setup_item(1, main[:, 1, :].rearrange("p (k c) -> p k c", k=KC), athf[:, 0, :, :],
                       ath[:, 1, :, :])
            with dve.Fori(0, KC // 2) as i:
                for b in range(2):
                    at = bass.ds(i * 2 * P + b * P, P)
                    setup_item(2 * i + b + 2, main[:, b, :].rearrange("p (k c) -> p k c", k=KC),
                               w2part(wf, 0)[:, :, at], w2part(wslots, 1)[:, :, at])
            dve.wait_ge(split_hi, 1)
            V.tensor_tensor(split[:, 0, 1, :, :], stage[:, 0, :].rearrange("p (k i) -> p k i", k=KC),
                            splitf[:, 0, 0, :, :], ALU.subtract).then_inc(split_lo, 1)
            dve.wait_ge(split_hi, 2)
            V.tensor_tensor(split[:, 1, 1, :, :], b1c[:, :].unsqueeze(2).broadcast_to((P, KC, P)),
                            splitf[:, 1, 0, :, :], ALU.subtract).then_inc(split_lo, 1)
            dve.wait_ge(prod_hi, 2)
            V.tensor_tensor(bwx[:, 1, 0:H], main[:, 0, :], bwxf[:, 0, 0:H], ALU.subtract)
            V.tensor_tensor(bwx[:, 1, H:HX], psg[:, 0:CL], bwxf[:, 0, H:HX], ALU.subtract).then_inc(prod_lo, 1)
            dve.wait_ge(prod, 2)
            V.tensor_tensor(biasx[:, 0:H], main[:, 1, :], biasx[:, 0:H], ALU.add)
            V.tensor_copy(biasx[:, H:HX], psg[:, CL:2 * CL]).then_inc(prod_lo, 1)

            def quantise(i, b, two):
                t = 4 * i + two + b
                dve.wait_ge(x_in[b], 32 * i + 8 * two + 16)
                xt = xa[:, b, :]
                for sel, first in ((inv_sel, par2[:, 1, 0:1]), (low_sel, par2[:, 2, 0:1]),
                                   (del_sel, par[:, 1, 0:1])):
                    chain(V.tensor_copy(sel[:, :], first.broadcast_to((P, H))))
                chain(V.tensor_scalar(steps[:, :].bitcast(I32), xt.bitcast(I32), 0x7FFFFFFF, None,
                                      ALU.bitwise_and))
                for g in range(1, G + 1):
                    chain(V.tensor_scalar(mask[:, :], steps[:, :], par2[:, 0, g - 1:g], None, ALU.is_le))
                    dve.sem_inc(mask_seen, 1)
                    if g < G:
                        V.copy_predicated(inv_sel[:, :], mask[:, :], par2[:, 1, g:g + 1].broadcast_to((P, H)))
                        V.copy_predicated(del_sel[:, :], mask[:, :], par[:, 1, g:g + 1].broadcast_to((P, H)))
                        chain(V.copy_predicated(low_sel[:, :], mask[:, :],
                                                par2[:, 2, g:g + 1].broadcast_to((P, H))))
                    else:
                        V.copy_predicated(inv_sel[:, :], mask[:, :], edge[:, 0:1].broadcast_to((P, H)))
                        chain(V.copy_predicated(low_sel[:, :], mask[:, :], edge[:, 1:2].broadcast_to((P, H))))
                chain(V.tensor_tensor(steps[:, :], xt, inv_sel[:, :], ALU.mult))
                chain(V.tensor_scalar(steps[:, :], steps[:, :], ROUND, ROUND, ALU.add, ALU.subtract))
                chain(V.tensor_tensor(steps[:, :], steps[:, :], low_sel[:, :], ALU.max))
                chain(V.scalar_tensor_tensor(steps[:, :], low_sel[:, :], LEVELS - 1.0, steps[:, :],
                                             ALU.add, ALU.min))
                dve.wait_ge(q_free, t + 1)
                V.tensor_tensor(qrow[:, b, :], steps[:, :], del_sel[:, :], ALU.mult).then_inc(q_ready, 1)

            first, per = chain.here(), 4 * (4 + 2 * G + 4)
            with dve.Fori(0, KC // 2) as i:
                chain.turn(i, first, per)
                for b in range(2):
                    j = 2 * i + b
                    dve.wait_ge(split_hi, j + 3)
                    V.tensor_tensor(split[:, b, 1, :, :], stage[:, 1 - b, :].rearrange("p (k i) -> p k i", k=KC),
                                    splitf[:, b, 0, :, :], ALU.subtract).then_inc(split_lo, 1)
                    quantise(i, 0, 2 * b)
                    dve.wait_ge(prod_hi, 2 * j + 4)
                    V.tensor_tensor(mev[:, 1, 0:H], main[:, b, :], mevf[:, 0, 0:H], ALU.subtract)
                    V.tensor_tensor(mev[:, 1, H:HX], psg[:, b * CL:(b + 1) * CL], mevf[:, 0, H:HX],
                                    ALU.subtract).then_inc(prod_lo, 1)
                    quantise(i, 1, 2 * b)
                assert chain.n == per
            chain.turn(0, first + per * (KC // 2), 0)

            dve.wait_ge(gate_out, NT + 1)

            def best(logits, hot, top):
                wide = rcol[:, top, :].unsqueeze(2).broadcast_to((P, NT, E))
                chain(V.tensor_reduce(rcol[:, top, :], logits, axis=AX.X, op=ALU.max))
                chain(V.tensor_tensor(rbuf[:, 1, :, :], logits, wide, ALU.is_equal))
                chain(V.tensor_tensor(rbuf[:, 1, :, :], rbuf[:, 1, :, :],
                                      sc[:, 6:7, :].broadcast_to((P, NT, E)), ALU.mult))
                chain(V.tensor_reduce(rcol[:, 4, :], rbuf[:, 1, :, :], axis=AX.X, op=ALU.max))
                chain(V.tensor_tensor(hot, rbuf[:, 1, :, :],
                                      rcol[:, 4, :].unsqueeze(2).broadcast_to((P, NT, E)), ALU.is_equal))

            best(rbuf[:, 0, :, :], rbuf[:, 2, :, :], 0)
            chain(V.scalar_tensor_tensor(rbuf[:, 4, :, :], rbuf[:, 2, :, :], -3.0e38, rbuf[:, 0, :, :],
                                         ALU.mult, ALU.add))
            best(rbuf[:, 4, :, :], rbuf[:, 3, :, :], 1)
            V.tensor_tensor(rcol[:, 2, :], rcol[:, 1, :], rcol[:, 0, :], ALU.subtract).then_inc(exp_in, 1)
            V.tensor_tensor(hotB[:, 0, :].rearrange("p (t e) -> p t e", e=E), rbuf[:, 2, :, :],
                            rbuf[:, 3, :, :], ALU.add).then_inc(hots_ready, 1)
            dve.wait_ge(exp_out, 1)
            chain(V.tensor_scalar(rcol[:, 5, :], rcol[:, 3, :], 1.0, None, ALU.add))
            chain(V.reciprocal(wts[:, 0, :], rcol[:, 5, :]))
            V.tensor_tensor(wts[:, 1, :], rcol[:, 3, :], wts[:, 0, :], ALU.mult)

            def scan(a, b, n, at):
                shift = 1
                while shift < n:
                    V.tensor_copy(at(b, 0, shift), at(a, 0, shift))
                    chain(V.tensor_tensor(at(b, shift, n), at(a, shift, n), at(a, 0, n - shift), ALU.add))
                    a, b, shift = b, a, 2 * shift
                return a

            dve.wait_ge(counted, 1)
            chain(V.tensor_copy(rbuf[:, 5, :, :], psg[:, 0:P].rearrange("p (t e) -> p t e", e=E)))
            chain(V.tensor_copy(rbuf[:, 6, :, :], rbuf[:, 5, :, :]))
            s = scan(6, 7, NT, lambda buf, lo, hi: rbuf[:, buf, lo:hi, :])
            chain(V.tensor_tensor(rbuf[:, 8, :, :], rbuf[:, s, :, :], rbuf[:, 5, :, :], ALU.subtract))
            chain(V.tensor_tensor(rbuf[:, 8, :, :], rbuf[:, 8, :, :],
                                  psl[:, 0:P].rearrange("p (t e) -> p t e", e=E), ALU.add))
            chain(V.tensor_scalar(tint[:, :], rbuf[:, s, NT - 1, :], P - 1.0, None, ALU.add))
            chain(V.tensor_scalar(tint[:, :], tint[:, :], 7, None, ALU.logical_shift_right))
            chain(V.tensor_copy(sc[:, 0, :], tint[:, :]))
            chain(V.tensor_copy(sc[:, 1, :], sc[:, 0, :]))
            s = scan(1, 2, E, lambda buf, lo, hi: sc[:, buf, lo:hi])
            ends = sc[:, s, :]
            chain(V.tensor_tensor(sc[:, 3, :], ends, sc[:, 0, :], ALU.subtract))
            chain(V.scalar_tensor_tensor(rbuf[:, 9, :, :], sc[:, 3:4, :].broadcast_to((P, NT, E)), float(P),
                                         rbuf[:, 8, :, :], ALU.mult, ALU.add))
            for n in range(2):
                chain(V.tensor_tensor(rbuf[:, 4 + n, :, :], rbuf[:, 9, :, :], rbuf[:, 2 + n, :, :], ALU.mult))
                chain(V.tensor_reduce(slots[:, n, :], rbuf[:, 4 + n, :, :], axis=AX.X, op=ALU.add))
            V.tensor_copy(slotu[:, :, :], slots[:, :, :])
            chain(V.tensor_copy(sli[:, :, :], slots[:, :, :]))
            chain(V.tensor_scalar(sli2[:, 0, :, :], sli[:, :, :], 7, None, ALU.logical_shift_right))
            chain(V.tensor_scalar(sli2[:, 1, :, :], sli[:, :, :], P - 1, None, ALU.bitwise_and))
            V.tensor_copy(shi[:, :, :], sli2[:, 0, :, :])
            chain(V.tensor_copy(slo[:, :, :], sli2[:, 1, :, :]))
            n2 = 2 * NT
            flat = lambda a: a.rearrange("p n t -> p (n t)")
            V.tensor_tensor(hotB[:, :, :], rowi[:, :].unsqueeze(1).broadcast_to((P, n2, P)),
                            flat(slo[:, :, :]).unsqueeze(2).broadcast_to((P, n2, P)), ALU.is_equal)
            chain(V.tensor_tensor(hotA[:, :, :], mt_row[:, :].unsqueeze(1).broadcast_to((P, n2, MT)),
                                  flat(shi[:, :, :]).unsqueeze(2).broadcast_to((P, n2, MT)), ALU.is_equal))
            V.tensor_scalar(hotX[:, :, 0:MT], hotA[:, :, :], parti[:, :], None, ALU.mult)
            V.tensor_tensor(hotX[:, :, MT:2 * MT], hotA[:, :, :],
                            flat(tcol[:, :, :]).unsqueeze(2).broadcast_to((P, n2, MT)),
                            ALU.mult).then_inc(slots_ready, 1)
            chain(V.tensor_tensor(mt_cmp[:, :, :], mt_row[:, :].unsqueeze(2).broadcast_to((P, MT, E - 1)),
                                  ends[:, 0:E - 1].unsqueeze(1).broadcast_to((P, MT, E - 1)), ALU.is_ge))
            chain(V.tensor_reduce(mt_exp[:, :], mt_cmp[:, :, :], axis=AX.X, op=ALU.add))
            V.tensor_scalar(mt_need[:, :], mt_exp[:, :], 1.0, float(KC), ALU.max, ALU.mult)
            chain(V.tensor_scalar(mt_cmp[:, :, 1], mt_exp[:, :], 1.0, float(KC), ALU.min, ALU.mult))
            V.tensor_scalar(mt_need1[:, :], mt_cmp[:, :, 1], 1.0, None, ALU.add)
            V.tensor_scalar(freeat[:, 2:E + 1], ends[:, 0:E - 1], 1.0, None, ALU.add)
            chain(V.tensor_copy(mt_int[:, :], mt_exp[:, :]))
            chain(V.tensor_scalar(mt_int[:, :], mt_int[:, :], 1, None, ALU.bitwise_and))
            chain(V.tensor_copy(mt_exp[:, :], mt_int[:, :]))
            chain(V.tensor_scalar(mt_par[:, :], mt_exp[:, :], float(SLOT1), None, ALU.mult))
            dve.wait_ge(placed, 1)
            chain(V.tensor_copy(mt_cmp[:, :, 0], psg[:, 0:MT]))
            V.scalar_tensor_tensor(toku[:, :], psg[:, MT:2 * MT], float(P), mt_cmp[:, :, 0], ALU.mult,
                                   ALU.add).then_inc(routed, 1)

            def take(s, b):
                dve.wait_ge(t_T, s + 1)
                if not (isinstance(s, int) and s == 0):
                    dve.wait_ge(tile_done, s)
                V.tensor_copy(split[:, b, 0, :, :], pst[:, :, :]).then_inc(t_split, 1)
                dve.wait_ge(t_split, 2 * s + 1)
                V.tensor_tensor(split[:, b, 1, :, :], pst[:, :, :], splitf[:, b, 0, :, :],
                                ALU.subtract).then_inc(t_split, 1)

            def give(i, s, b):
                dve.wait_ge(tile_done, s + 2)
                if not (isinstance(i, int) and i == 0):
                    dve.wait_ge(y_store[b], 16 * i)
                V.tensor_copy(yout[:, b, :], main[:, b, :]).then_inc(y_out, 1)

            take(0, 0)
            take(1, 1)
            for c in range(KC):
                dve.wait_ge(wch_hi, KC + c + 1)
                V.tensor_tensor(expart(wslots, 1, 1)[:, c, :], stage[:, c % 4, :],
                                expart(wf, 1, 0)[:, c, :], ALU.subtract).then_inc(one_lo, 1)
            give(0, 0, 0)
            take(2, 0)
            give(0, 1, 1)
            with dve.Fori(1, MT // 2) as i:
                take(2 * i + 1, 1)
                give(i, 2 * i, 0)
                take(2 * i + 2, 0)
                give(i, 2 * i + 1, 1)
            give(MT // 2, MT - 1, 0)

            dve.wait_ge(y_store[0], 16 * (MT // 2 + 1))
            dve.wait_ge(y_store[1], 16 * (MT // 2))

            def total(i, b, t):
                dve.wait_ge(xc_in[b], 16 * i + 16)
                dve.wait_ge(ga_in[b], 16 * i + 16)
                dve.wait_ge(gb_in[b], 16 * i + 16)
                if not (isinstance(i, int) and i == 0):
                    dve.wait_ge(x1_store[b], 16 * i)
                at = (lambda n: wts[:, n, t:t + 1]) if isinstance(t, int) else (
                    lambda n: wts[:, n, bass.ds(t, 1)])
                chain(V.scalar_tensor_tensor(yout[:, b, :], gring[:, b, :], at(0), stage[:, b, :],
                                             ALU.mult, ALU.add))
                V.scalar_tensor_tensor(yout[:, b, :], tin[:, b, :], at(1), yout[:, b, :],
                                       ALU.mult, ALU.add).then_inc(x1_ready, 1)

            def layer(i, b, t):
                dve.wait_ge(x1_hi, t + 1)
                V.tensor_tensor(split[:, b, 1, :, :], pst[:, :, :], splitf[:, b, 0, :, :],
                                ALU.subtract).then_inc(x1_lo, 1)
                dve.wait_ge(low_done, t + 1)
                V.tensor_scalar(lows[:, :], psl[:, 0:P], comb[:, bass.ds(i, 1)], None,
                                ALU.mult).then_inc(low_scaled, 1)
                dve.wait_ge(low_hi, t + 1)
                V.tensor_tensor(lowr[:, 1, :], lows[:, :], lowrf[:, 0, :], ALU.subtract).then_inc(low_lo, 1)

            def judge(t, b):
                dve.wait_ge(layer_done, t + 1)
                V.tensor_tensor(zl[:, :], psg[:, 0:CL], biasx[:, H:HX], ALU.add).then_inc(scores_out, 1)
                dve.wait_ge(scores_out, t + 2)
                chain(V.tensor_reduce(smx[:, 0:1], zl[:, :], axis=AX.X, op=ALU.max))
                V.tensor_scalar(smx[:, 1:2], smx[:, 0:1], -1.0 / TEMPERATURE, None, ALU.mult).then_inc(nb_ready, 1)
                V.tensor_tensor(dense[:, t, :] if isinstance(t, int) else
                                dense[:, bass.ds(t, 1), :].rearrange("p o n -> p (o n)"),
                                main[:, b, :], biasx[:, 0:H], ALU.add).then_inc(dense_out, 1)
                dve.wait_ge(soft_done, t + 1)
                chain(V.reciprocal(smx[:, 3:4], smx[:, 2:3]))
                chain(V.tensor_scalar(hits[:, :], el[:, :], smx[:, 3:4], THRESHOLD, ALU.mult, ALU.is_gt))
                V.tensor_reduce(qsel[:, t:t + 1] if isinstance(t, int) else qsel[:, bass.ds(t, 1)],
                                hits[:, :], axis=AX.X, op=ALU.max)
                chain(V.tensor_tensor(cacc[:, :], cacc[:, :], hits[:, :], ALU.max))

            total(0, 0, 0)
            layer(0, 0, 0)
            total(0, 1, 1)
            judge(0, 0)
            layer(0, 1, 1)
            first, per = chain.here(), 10
            with dve.Fori(1, NT // 2) as i:
                chain.turn(i - 1, first, per)
                total(i, 0, 2 * i)
                judge(2 * i - 1, 1)
                layer(i, 0, 2 * i)
                total(i, 1, 2 * i + 1)
                judge(2 * i, 0)
                layer(i, 1, 2 * i + 1)
                assert chain.n == per, chain.n
            chain.turn(0, first + per * (NT // 2 - 1), 0)
            judge(NT - 1, 1)

            V.tensor_copy(caccb[:, :], cacc[:, :]).then_inc(cacc_ready, 1)
            dve.wait_ge(clu_done, 1)
            chain(V.tensor_copy(clu[:, :], psl[0:CL, 0:1]))
            V.tensor_scalar(cselb[:, :], ones[0:CL, :], clu[:, :], 0.5, ALU.mult, ALU.is_gt
                            ).then_inc(csel_ready, 1)
            dve.wait_ge(rowsel_done, 1)
            chain(V.tensor_copy(gring[:, 0, :], main[:, 0, :]))

            def finish(i, c, t):
                dve.wait_ge(xr_in[c], 16 * i + 16)
                if not (isinstance(i, int) and i == 0 and c < 2):
                    dve.wait_ge(out_store[c % 2], 32 * i + 16 * (c // 2))
                one = dense[:, t, :] if isinstance(t, int) else dense[:, bass.ds(t, 1), :].rearrange("p o n -> p (o n)")
                pick = qsel[:, t:t + 1] if isinstance(t, int) else qsel[:, bass.ds(t, 1)]
                chain(V.scalar_tensor_tensor(tin[:, c % 2, :], one, pick, gring[:, 0, :], ALU.mult, ALU.mult))
                V.tensor_tensor(yout[:, c % 2, :], tin[:, c % 2, :], stage[:, c, :], ALU.add).then_inc(fin_ready, 1)

            for c in range(4):
                finish(0, c, c)
            first, per = chain.here(), 4
            with dve.Fori(1, NT // 4) as i:
                chain.turn(i - 1, first, per)
                for c in range(4):
                    finish(i, c, 4 * i + c)
                assert chain.n == per
            chain.turn(0, first + per * (NT // 4 - 1), 0)

        @block.tensor
        def _(pe):
            def mm(o, l, r, start, stop):
                return nc.tensor.matmul(o, l, r, start=start, stop=stop)

            def three(cols, stationary, moving):
                for k in range(KC):
                    for sp_, mp in ((0, 0), (0, 1), (1, 0)):
                        for o, lo, hi in cols:
                            last = mm(o, stationary(k, sp_), moving(k, mp, lo, hi),
                                      k == 0 and (sp_, mp) == (0, 0), k == KC - 1 and (sp_, mp) == (1, 0))
                return last

            pe.wait_ge(iota_done, 2)
            pe.wait_ge(stage_in[0], 16)
            for k in range(KC):
                last = nc.tensor.transpose(main[:, 0, k * CL:(k + 1) * CL], stage[0:CL, 0, k * P:(k + 1) * P],
                                           ident[0:CL, 0:CL])
            last.then_inc(setup_T, 1)
            pe.wait_ge(stage_in[1], 16)
            for k in range(KC):
                last = nc.tensor.transpose(main[:, 1, k * P:(k + 1) * P], stage[:, 1, k * P:(k + 1) * P],
                                           ident[:, :])
            last.then_inc(setup_T, 1)
            with pe.Fori(0, KC // 2) as i:
                for b in range(2):
                    pe.wait_ge(stage_in[b], 16 * i + 32)
                    pe.wait_ge(setup_lo, 2 * i + b + 1)
                    for k in range(KC):
                        last = nc.tensor.transpose(main[:, b, k * P:(k + 1) * P],
                                                   stage[:, b, k * P:(k + 1) * P], ident[:, :])
                    last.then_inc(setup_T, 1)
            pe.wait_ge(setup_lo, KC + 2)

            def product(m, b):
                pe.wait_ge(split_lo, m + 1)
                last = three([(main[:, b, 0:NB], 0, NB), (main[:, b, NB:H], NB, H),
                              (psg[:, b * CL:(b + 1) * CL], H, HX)],
                             lambda k, part: split[:, b, part, k, :],
                             lambda k, part, lo, hi: w2part(wslots, part)[:, k, lo:hi])
                last.then_inc(prod, 1)

            product(0, 0)
            pe.wait_ge(prod_lo, 1)
            product(1, 1)
            pe.wait_ge(consts, 1)

            def tile(t, b):
                pe.wait_ge(q_ready, t + 1)
                for k in range(KC):
                    last = nc.tensor.transpose(pst[:, k, :], qrow[:, b, k * P:(k + 1) * P], ident[:, :])
                last.then_inc(q_T, 1)
                pe.wait_ge(q_Tout, t + 1)
                pe.wait_ge(gate_out, t + 1)
                for k in range(KC):
                    last = mm(psl[:, 0:E], qT[:, k, :], gw[:, k, :], k == 0, k == KC - 1)
                last.then_inc(gate, 1)

            with pe.Fori(0, KC // 2) as i:
                for b in range(2):
                    pe.wait_ge(prod_lo, 2 * i + b + 2)
                    product(2 * i + b + 2, b)
                    tile(4 * i + 2 * b, 0)
                    tile(4 * i + 2 * b + 1, 1)

            pe.wait_ge(prod_lo, KC + 2)
            pe.wait_ge(gate_out, NT + 1)
            pe.wait_ge(hots_ready, 1)
            mm(psl[:, 0:P], tri[:, :], hotB[:, 0, :], True, True)
            mm(psg[:, 0:P], ones[:, :], hotB[:, 0, :], True, True).then_inc(counted, 1)
            pe.wait_ge(slots_ready, 1)
            for n in range(2 * NT):
                last = mm(psg[:, 0:2 * MT], hotB[:, n, :], hotX[:, n, :], n == 0, n == 2 * NT - 1)
            last.then_inc(placed, 1)
            pe.wait_ge(routed, 1)

            def turn_rows(nth, s, b):
                pe.wait_ge(tin_in[b], 16 * nth)
                for k in range(KC):
                    last = nc.tensor.transpose(pst[:, k, :], tin[:, b, k * P:(k + 1) * P], ident[:, :])
                last.then_inc(t_T, 1)

            def multiply(s, b):
                at = (lambda tab: tab[0:1, s:s + 1]) if isinstance(s, int) else (
                    lambda tab: tab[0:1, bass.ds(s, 1)])
                need = pe.value_load(at(mt_need), min_val=KC, max_val=E * KC)
                need1 = pe.value_load(at(mt_need1), min_val=1, max_val=KC + 1)
                base = pe.value_load(at(mt_par), min_val=0, max_val=SLOT1)
                pe.wait_ge(wch_lo, need)
                pe.wait_ge(one_lo, need1)
                pe.wait_ge(y_out, s + 1)
                last = three([(main[:, b, 0:NB], 0, NB), (main[:, b, NB:H], NB, H)],
                             lambda k, part: split[:, b, part, k, :],
                             lambda k, part, lo, hi: wslots[:, bass.ds(base + part * WE + k * H + lo, hi - lo)])
                last.then_inc(tile_done, 1)

            turn_rows(1, 0, 0)

            def turn(i):
                pe.wait_ge(t_split, 4 * i + 2)
                turn_rows(i + 1, 2 * i + 1, 1)
                multiply(2 * i, 0)
                pe.wait_ge(t_split, 4 * i + 4)
                turn_rows(i + 2, 2 * i + 2, 0)
                multiply(2 * i + 1, 1)

            with pe.Fori(0, MT // 2) as i:
                turn(i)
            pe.wait_ge(t_split, 2 * MT)
            multiply(MT - 1, 0)

            pe.wait_ge(m_in, 32)
            pe.wait_ge(y_out, MT + 2)

            def turn_x1(t, b):
                pe.wait_ge(x1_ready, t + 3)
                for k in range(KC):
                    last = nc.tensor.transpose(pst[:, k, :], yout[:, b, k * P:(k + 1) * P], ident[:, :])
                last.then_inc(x1_T, 1)

            def layer(t, b, more):
                pe.wait_ge(x1_lo, t + 1)
                last = three([(psl[:, 0:P], 0, P)], lambda k, part: ath[:, part, k, :],
                             lambda k, part, lo, hi: split[:, b, part, k, lo:hi])
                last.then_inc(low_done, 1)
                pe.wait_ge(dense_out, t + 1)
                cols = [(main[:, b, 0:NB], 0, NB), (main[:, b, NB:H], NB, H), (psg[:, 0:CL], H, HX)]
                for part in (cols[:2], cols[2:]):
                    if part[0][1] == H:
                        pe.wait_ge(scores_out, t + 1)
                    for k in range(KC):
                        for sp_, mp in ((0, 0), (0, 1), (1, 0)):
                            for o, lo, hi in part:
                                mm(o, split[:, b, sp_, k, :], w2part(wslots, mp)[:, k, lo:hi],
                                   k == 0 and (sp_, mp) == (0, 0), False)
                if more:
                    turn_x1(t + 1, 1 - b)
                pe.wait_ge(low_lo, t + 1)
                for sp_, mp in ((0, 0), (0, 1), (1, 0)):
                    for o, lo, hi in cols:
                        last = mm(o, lowr[:, sp_, :], bwx[:, mp, lo:hi], False, (sp_, mp) == (1, 0))
                last.then_inc(layer_done, 1)

            turn_x1(0, 0)
            layer(0, 0, True)
            with pe.Fori(0, NT // 2 - 1) as i:
                layer(2 * i + 1, 1, True)
                layer(2 * i + 2, 0, True)
            layer(NT - 1, 1, False)

            pe.wait_ge(cacc_ready, 1)
            mm(psl[0:CL, 0:1], caccb[:, :], ones[:, 0:1], True, True).then_inc(clu_done, 1)
            pe.wait_ge(csel_ready, 1)
            mm(main[:, 0, 0:NB], cselb[:, :], pickT[:, 0:NB], True, True)
            mm(main[:, 0, NB:H], cselb[:, :], pickT[:, NB:H], True, True).then_inc(rowsel_done, 1)


_INS = ["x", "condB_thresholds", "condB_deltas", "condB_zeropoints", "itok_B_1_7", "L0_ffn_gate_w",
        "L0_ffn_expert_w", "L1_cond_weight", "L1_cond_bias", "L1_cond_lora_a_weights",
        "L1_cond_lora_b_weights", "L1_cond_scaling_factors", "L1_ffn_weight", "L1_ffn_bias",
        "L1_ffn_centroids", "L1_ffn_assignments"]


def kernel(**inputs):
    import concourse.bacc as bacc
    from concourse.bass_utils import run_bass_kernel_spmd

    nc = bacc.Bacc("TRN2", target_bir_lowering=False, num_devices=1, dynamic_dma_scratch_size=4096)
    arrays, args = {}, []
    for name in _INS:
        a = np.ascontiguousarray(inputs[name])
        if name == "x":
            a = a.reshape(TOK, H)
        arrays[f"in_{name}"] = a
        args.append(nc.dram_tensor(f"in_{name}", a.shape, mybir.dt.from_np(a.dtype), kind="ExternalInput").ap())
    out = nc.dram_tensor("out", [TOK, H], F32, kind="ExternalOutput").ap()
    build(nc, *args, out)
    r = run_bass_kernel_spmd(nc, [arrays], core_ids=[0])
    return r.results[0]["out"].reshape(inputs["x"].shape)
```

```python
from contextlib import ExitStack

import numpy as np

import concourse.bass as bass
from concourse import mybir

F32 = mybir.dt.float32
F32R = mybir.dt.float32r
BF16 = mybir.dt.bfloat16
I32 = mybir.dt.int32
U32 = mybir.dt.uint32
U8 = mybir.dt.uint8
ALU = mybir.AluOpType
ACT = mybir.ActivationFunctionType
AX = mybir.AxisListType

P = 128
H = 1024
KC = H // P
TOK = 2048
NT = TOK // P
E = 8
TOPK = 2
G = 8
LEVELS = 64
OWN = 3
RING = 4
CL = 64
HX = H + CL
R = 16
A = 8
MT = TOK * TOPK // P + E - 1
NB = 512
W2X = KC * HX
WE = KC * H
SLOT1 = 2 * W2X
ROUND = 1.5 * 2.0 ** 23
TEMPERATURE = 0.1
THRESHOLD = 0.01


class Chain:

    def __init__(self, engine, sem):
        self.engine, self.sem, self.base, self.n = engine, sem, 0, 0

    def __call__(self, instruction):
        self.n += 1
        instruction.then_inc(self.sem, 1)
        self.engine.wait_ge(self.sem, self.base + self.n)

    def turn(self, i, first, per):
        self.base, self.n = first + i * per, 0

    def here(self):
        return self.base + self.n


def build(nc, x, thresholds, deltas, zero_points, adapter, gate_w, expert_w, w1, b1, lora_a, lora_b,
          scaling, w2, b2, centroids, assignments, out):
    def scratch(name, shape, dt):
        return nc.dram_tensor(name, shape, dt).ap()

    q_dram = scratch("q_dram", [TOK, H], F32)
    y_dram = scratch("y_dram", [MT * P, H], F32)
    m_dram = scratch("m_dram", [2, P, KC, HX], F32)

    with ExitStack() as ctx:
        def sb(name, shape, dt=F32):
            return ctx.enter_context(nc.sbuf_tensor(name, shape, dt))

        def sem(name):
            return ctx.enter_context(nc.semaphore(name))

        with ExitStack() as under:
            def over(name, shape, dt=F32):
                return under.enter_context(nc.sbuf_tensor(name, shape, dt))
            over("under_slot0", [P, SLOT1])
            mev = over("mev", [P, 2, HX], F32R)
            qrow = over("qrow", [P, 2, H])
            qT = over("qT", [P, KC, P])
            rbuf = over("rbuf", [P, 10, NT, E])
            mt_cmp = over("mt_cmp", [P, MT, E - 1])
            rowi = over("rowi", [P, P])
            tri = over("tri", [P, P], BF16)
            gw = over("gw", [P, KC, E])
            par = over("par", [P, 4, G])
            par2 = over("par2", [P, 4, G])
            zero = over("zero", [P, 1])
            rnd = over("rnd", [P, 2])
            sc = over("sc", [P, 8, E])
            rcol = over("rcol", [P, 8, NT])
            slots = over("slots", [P, 2, NT])
            sli = over("sli", [P, 2, NT], I32)
            sli2 = over("sli2", [P, 2, 2, NT], I32)
            slo = over("slo", [P, 2, NT])
            shi = over("shi", [P, 2, NT])
            tcol = over("tcol", [P, 2, NT])
            mt_row = over("mt_row", [P, MT])
            mt_exp = over("mt_exp", [P, MT])
            mt_int = over("mt_int", [P, MT], I32)
            tint = over("tint", [P, E], I32)
            with ExitStack() as inner:
                def first(name, shape, dt=F32):
                    return inner.enter_context(nc.sbuf_tensor(name, shape, dt))
                xa = first("xa", [P, 2, H])
                some = first("some", [P, 4, H])
                mask = first("mask", [P, 4, H], U8)
            hotB = over("hotB", [P, 2 * NT, P], BF16)
            hotA = over("hotA", [P, 2 * NT, MT], BF16)
            hotX = over("hotX", [P, 2 * NT, 2 * MT], BF16)
        with ExitStack() as under:
            under.enter_context(nc.sbuf_tensor("under_slot0b", [P, SLOT1], F32))
            x1 = under.enter_context(nc.sbuf_tensor("x1", [P, NT, H], F32))
        wslots = sb("wslots", [P, 2 * W2X + 2 * WE], F32R)
        ath = sb("ath", [P, 2, KC, P], F32R)
        bwx = sb("bwx", [P, 2, HX], F32R)
        split = sb("split", [P, 2, 2, KC, P], F32R)
        stage = sb("stage", [P, RING, H])
        gring = sb("gring", [P, 2, H])
        tin = sb("tin", [P, 2, H])
        yout = sb("yout", [P, 2, H])
        biasx = sb("biasx", [P, HX])
        pickT = sb("pickT", [CL, H], BF16)
        ident = sb("ident", [P, P])
        parti = sb("parti", [P, 1])
        ones = sb("ones", [P, P], BF16)
        b1c = sb("b1c", [P, KC])
        adp = sb("adp", [P, E], I32)
        adpf = sb("adpf", [P, E])
        comb = sb("comb", [P, E])
        wts = sb("wts", [P, 2, NT])
        idx = sb("idx", [P, 2, 2], U32)
        slotu = sb("slotu", [P, 2, NT], U32)
        mt_par = sb("mt_par", [P, MT], I32)
        mt_need = sb("mt_need", [P, MT], I32)
        freeat = sb("freeat", [P, E + 1], I32)
        toku = sb("toku", [P, MT], U32)
        lows = sb("lows", [P, 2 * P])
        lowr = sb("lowr", [P, 2, 2 * P], F32R)
        negi = sb("negi", [P, P], F32R)
        scT = sb("scT", [P, 2 * P])
        zl = sb("zl", [P, 2, CL])
        el = sb("el", [P, 2, CL])
        hits = sb("hits", [P, 2, CL])
        cacc = sb("cacc", [P, CL])
        caccb = sb("caccb", [P, CL], BF16)
        smx = sb("smx", [P, 4, 2])
        qsel = sb("qsel", [P, NT])
        cselb = sb("cselb", [CL, P], BF16)
        clu = sb("clu", [CL, 1])
        flag = sb("flag", [P, 1], I32)

        wf = wslots[:, :].bitcast(F32)
        splitf = split[:, :, :, :, :].bitcast(F32)
        athf = ath[:, :, :, :].bitcast(F32)
        bwxf = bwx[:, :, :].bitcast(F32)
        mevf = mev[:, :, :].bitcast(F32)
        lowrf = lowr[:, :, :].bitcast(F32)

        bucket = [some[:, n, :] for n in range(4)] + [buf[:, n, :] for buf in (tin, yout) for n in range(2)]
        magnitude = stage[:, 2:4, :]

        def w2part(tensor, part):
            return tensor[:, part * W2X:(part + 1) * W2X].rearrange("p (k n) -> p k n", k=KC)

        def expart(tensor, odd, part):
            o = odd * SLOT1 + part * WE
            return tensor[:, o:o + WE].rearrange("p (k n) -> p k n", k=KC)

        main = ctx.enter_context(nc.psum_tensor("main", [P, 2, H], F32))
        pst = ctx.enter_context(nc.psum_tensor("pst", [P, KC, P], F32))
        psg = ctx.enter_context(nc.psum_tensor("psg", [P, NB], F32))
        psl = ctx.enter_context(nc.psum_tensor("psl", [P, NB], F32))

        const_in = sem("const_in")
        iota_done = sem("iota_done")
        consts = sem("consts")
        lora_in = sem("lora_in")
        stage_in = [sem(f"stage_in{i}") for i in range(4)]
        w1_in = [sem(f"w1_in{i}") for i in range(2)]
        setup_T = sem("setup_T")
        setup_hi = sem("setup_hi")
        setup_lo = sem("setup_lo")
        split_hi = sem("split_hi")
        split_lo = sem("split_lo")
        prod = sem("prod")
        prod_hi = sem("prod_hi")
        prod_lo = sem("prod_lo")
        m_free = sem("m_free")
        m_store = sem("m_store")
        x_in = [sem(f"x_in{i}") for i in range(2)]
        q_ready = sem("q_ready")
        q_store = [sem(f"q_store{i}") for i in range(2)]
        q_free = sem("q_free")
        x_used = sem("x_used")
        q_T = sem("q_T")
        q_Tout = sem("q_Tout")
        gate = sem("gate")
        gate_out = sem("gate_out")
        dve_chain = sem("dve_chain")
        exp_in = sem("exp_in")
        exp_out = sem("exp_out")
        hots_ready = sem("hots_ready")
        counted = sem("counted")
        slots_ready = sem("slots_ready")
        placed = sem("placed")
        routed = sem("routed")
        idx_ready = sem("idx_ready")
        idx_seen = sem("idx_seen")
        steps_ready = sem("steps_ready")
        ints_ready = sem("ints_ready")
        clipped = sem("clipped")
        scaled = sem("scaled")
        lower_done = sem("lower_done")
        picked = sem("picked")
        pick_seen = sem("pick_seen")
        zero_hi = sem("zero_hi")
        zero_lo = sem("zero_lo")
        exp_hi = sem("exp_hi")
        exp_lo = sem("exp_lo")
        tin_in = [sem(f"tin_in{i}") for i in range(2)]
        t_T = sem("t_T")
        t_hi = sem("t_hi")
        t_rest = sem("t_rest")
        t_lo = sem("t_lo")
        tile_done = sem("tile_done")
        y_out = sem("y_out")
        y_store = [sem(f"y_store{i}") for i in range(2)]
        m_in = sem("m_in")
        xc_in = [sem(f"xc_in{i}") for i in range(2)]
        ga_in = [sem(f"ga_in{i}") for i in range(2)]
        gb_in = [sem(f"gb_in{i}") for i in range(2)]
        x1_ready = sem("x1_ready")
        x1_kept = sem("x1_kept")
        x1_T = sem("x1_T")
        x1_hi = sem("x1_hi")
        x1_lo = sem("x1_lo")
        low_done = sem("low_done")
        low_scaled = sem("low_scaled")
        low_hi = sem("low_hi")
        low_lo = sem("low_lo")
        layer_done = sem("layer_done")
        dense_out = sem("dense_out")
        scoresT = sem("scoresT")
        scT_out = sem("scT_out")
        scores = sem("scores")
        nb_ready = sem("nb_ready")
        soft_done = sem("soft_done")
        cacc_ready = sem("cacc_ready")
        clu_done = sem("clu_done")
        csel_ready = sem("csel_ready")
        rowsel_done = sem("rowsel_done")
        out_ready = sem("out_ready")
        flag_ready = sem("flag_ready")
        again_in = [sem(f"again_in{i}") for i in range(2)]
        again_ready = sem("again_ready")
        again_seen = sem("again_seen")
        again_free = sem("again_free")
        again_store = [sem(f"again_store{i}") for i in range(2)]
        out_store = [sem(f"out_store{i}") for i in range(2)]

        N_CONST = 9
        STAGED = (16 * (1 + KC // 2), 16 * (1 + KC // 2), 0, 0)
        block = ctx.enter_context(nc.Block())

        def rows(i):
            return slice(i * P, (i + 1) * P) if isinstance(i, int) else bass.ds(i * P, P)

        def tile_of(tensor, t):
            return tensor[:, t, :] if isinstance(t, int) else tensor[:, bass.ds(t, 1), :].rearrange(
                "p o n -> p (o n)")

        w1_v = w1.rearrange("(k p) (j i) -> j p k i", p=P, i=P)
        ew_v = expert_w.rearrange("e (k p) n -> (e k) p n", p=P)

        @block.sync
        def _(sp):
            sp.dma_start(stage[0:CL, 0, :], centroids).then_inc(stage_in[0], 16)
            sp.dma_start(stage[:, 1, :], lora_a.rearrange("a r i -> (a r) i")).then_inc(stage_in[1], 16)
            for n, source in enumerate((thresholds, deltas, zero_points, scaling)):
                sp.dma_start(par[:, n, :], source.partition_broadcast(P)).then_inc(const_in, 16)
            sp.dma_start(adp[:, :], adapter.partition_broadcast(P)).then_inc(const_in, 16)
            sp.dma_start(gw[:, :, :], gate_w.rearrange("(k p) e -> p k e", p=P)).then_inc(const_in, 16)
            with nc.allow_non_contiguous_dma(reason="a small column"):
                sp.dma_start(b1c[:, :], b1.rearrange("(k p) -> p k", p=P)).then_inc(const_in, 16)
            sp.dma_start(biasx[:, 0:H], b2.partition_broadcast(P)).then_inc(const_in, 16)
            sp.dma_start(gring[0:CL, 0, :].bitcast(I32),
                         assignments.partition_broadcast(CL)).then_inc(const_in, 16)
            for b in range(2):
                sp.dma_start(xa[:, b, :], x[rows(b), :]).then_inc(x_in[b], 16)
            with sp.Fori(0, KC // 2) as i:
                for b in range(2):
                    sp.wait_ge(setup_T, 2 * i + b + 1)
                    sp.dma_start(stage[:, b, :], w2[rows(2 * i + b), :]).then_inc(stage_in[b], 16)
            sp.wait_ge(setup_T, 2 + KC - 1)
            for k in range(KC):
                sp.dma_start(stage[:, 0, k * P:(k + 1) * P].rearrange("p (a r) -> p a r", a=A),
                             lora_b[:, k * P:(k + 1) * P, :].rearrange("a p r -> p a r")
                             ).then_inc(lora_in, 16)

            def quantised(i, more):
                for b in range(2):
                    sp.wait_ge(q_ready, 2 * i + b + 1)
                    sp.dma_start(q_dram[rows(2 * i + b), :], qrow[:, b, :]).then_inc(q_store[b], 16)
                    if more:
                        sp.dma_start(xa[:, b, :], x[rows(2 * i + b + 2), :]).then_inc(x_in[b], 16)

            with sp.Fori(0, NT // 2 - 1) as i:
                quantised(i, True)
            quantised(NT // 2 - 1, False)

            def fetch(n, c):
                sp.dma_start(stage[:, c, :], ew_v[n] if isinstance(n, int) else
                             ew_v[bass.ds(n, 1)].rearrange("o p n -> p (o n)")).then_inc(stage_in[c], 16)

            sp.wait_ge(split_lo, KC + 2)
            for n in range(RING + KC):
                if n >= RING:
                    sp.wait_ge(zero_lo, n - RING + 1)
                fetch(n, n % RING)
            with sp.Fori(1 + KC // RING, E * KC // RING) as r:
                for c in range(RING):
                    sp.wait_ge(exp_lo, RING * r + c - RING - KC + 2)
                    fetch(RING * r + c, c)

            sp.wait_ge(routed, 1)
            need = sp.value_load(freeat[0:1, E:E + 1], min_val=1, max_val=MT + 1)
            sp.wait_ge(tile_done, need)
            sp.wait_ge(m_store, 16 * KC)
            sp.wait_ge(exp_lo, (E - 1) * KC + 1)
            for part in range(2):
                sp.dma_start(w2part(wf, part), m_dram[part]).then_inc(m_in, 16)

            def load(t, b):
                sp.dma_start(stage[:, b, :], x[rows(t), :]).then_inc(xc_in[b], 16)

            def store(t, b):
                sp.wait_ge(out_ready, t + 1)
                sp.dma_start(out[rows(t), :], yout[:, b, :]).then_inc(out_store[b], 16)

            for b in range(2):
                load(b, b)
            with sp.Fori(0, NT // 2 - 1) as i:
                for b in range(2):
                    sp.wait_ge(x1_ready, 2 * i + b + 3)
                    load(2 * i + b + 2, b)
                for b in range(2):
                    store(2 * i + b, b)
            for b in range(2):
                store(NT - 2 + b, b)
            for b in range(2):
                sp.wait_ge(out_store[b], 16 * NT // 2)

            sp.wait_ge(flag_ready, 1)
            whole = sp.value_load(flag[0:1, 0:1], min_val=0, max_val=1)
            with sp.If(whole < 1):
                sp.sem_inc(again_free, 2)
                for b in range(2):
                    sp.dma_start(yout[:, b, :], out[rows(b), :]).then_inc(again_in[b], 16)

                def again(i, more):
                    for b in range(2):
                        sp.wait_ge(again_ready, 2 * i + b + 1)
                        sp.dma_start(out[rows(2 * i + b), :], tin[:, b, :]).then_inc(again_store[b], 16)
                        sp.wait_ge(again_store[b], 16 * i + 16)
                        sp.sem_inc(again_free, 1)
                        if more:
                            sp.dma_start(yout[:, b, :], out[rows(2 * i + b + 2), :]).then_inc(again_in[b], 16)

                with sp.Fori(0, NT // 2 - 1) as i:
                    again(i, True)
                again(NT // 2 - 1, False)
                for b in range(2):
                    sp.wait_ge(again_store[b], 16 * NT // 2)

        @block.gpsimd
        def _(pool):
            nc.gpsimd.memset(ident[:, :], 0.0).then_inc(iota_done, 1)
            pool.wait_ge(iota_done, 1)
            nc.gpsimd.affine_select(out=ident[:, :], in_=ident[:, :], compare_op=ALU.not_equal, fill=1.0,
                                    base=0, pattern=[[-1, P]], channel_multiplier=1).then_inc(iota_done, 1)
            kw = dict(allow_small_or_imprecise_dtypes=True)
            nc.gpsimd.iota(rowi[:, :], [[1, P]], base=0, channel_multiplier=0, **kw).then_inc(iota_done, 1)
            nc.gpsimd.iota(parti[:, :], [[0, 1]], base=0, channel_multiplier=1, **kw).then_inc(iota_done, 1)
            nc.gpsimd.iota(tcol[:, :, :], [[0, 2], [1, NT]], base=0, channel_multiplier=0,
                           **kw).then_inc(iota_done, 1)
            nc.gpsimd.iota(mt_row[:, :], [[1, MT]], base=0, channel_multiplier=0, **kw).then_inc(iota_done, 1)
            nc.gpsimd.memset(sc[:, 7, :], 1.0).then_inc(iota_done, 1)
            pool.wait_ge(iota_done, 7)
            nc.gpsimd.affine_select(out=sc[:, 7, :], in_=sc[:, 7, :], compare_op=ALU.is_ge, fill=0.0,
                                    base=0, pattern=[[-R, A]], channel_multiplier=1).then_inc(iota_done, 1)
            pool.wait_ge(iota_done, 8)
            nc.gpsimd.affine_select(out=sc[:, 7, :], in_=sc[:, 7, :], compare_op=ALU.is_ge, fill=0.0,
                                    base=R - 1, pattern=[[R, A]], channel_multiplier=-1).then_inc(iota_done, 1)
            nc.gpsimd.iota(sc[:, 6, :], [[-1, E]], base=E, channel_multiplier=0, **kw).then_inc(iota_done, 1)
            nc.gpsimd.iota(sc[:, 5, :], [[1, A]], base=0, channel_multiplier=0, **kw).then_inc(iota_done, 1)

            pool.sem_inc(m_free, 1)
            pool.wait_ge(setup_T, 2 + KC)

            def load(j, b):
                pool.wait_ge(split_lo, j + 1)
                pool.dma_start(stage[:, 1 - b, :].rearrange("p (k i) -> p k i", k=KC),
                               w1_v[j]).then_inc(w1_in[1 - b], 16)

            def store(j):
                pool.wait_ge(prod_lo, j + 3)
                pool.dma_start(m_dram[:, :, j, :].rearrange("h p n -> p h n"), mevf).then_inc(m_store, 16)
                pool.wait_ge(m_store, 16 * (j + 1))
                pool.sem_inc(m_free, 1)

            load(0, 0)
            for j in range(1, KC):
                load(j, j % 2)
                store(j - 1)
            store(KC - 1)

            for c in range(KC):
                pool.wait_ge(zero_hi, c + 1)
                nc.gpsimd.tensor_tensor(expart(wslots, 0, 1)[:, c, :], stage[:, c % RING, :],
                                        expart(wf, 0, 0)[:, c, :], ALU.subtract).then_inc(zero_lo, 1)

            pool.wait_ge(routed, 1)
            for b in range(2):
                pool.wait_ge(q_store[b], 16 * NT // 2)

            def gather(source, table, column, n, to, b, landed):
                copies[0] += 1
                nc.gpsimd.tensor_copy(idx[:, n, b:b + 1], table[:, column]).then_inc(idx_ready, 1)
                pool.wait_ge(idx_ready, copies[1] + copies[0])
                pool.sem_inc(idx_seen, 1)
                nc.gpsimd.indirect_dma_start(
                    out=to[:, b, :], out_offset=None, in_=source,
                    in_offset=bass.IndirectOffsetOnAxis(ap=idx[:, n, b:b + 1], axis=0)).then_inc(landed[b], 16)

            copies = [0, 0]
            for b in range(2):
                gather(q_dram, toku, slice(b, b + 1), 0, tin, b, tin_in)
            with pool.Fori(1, MT // 2) as i:
                copies[:] = [0, 2 * i]
                for b in range(2):
                    pool.wait_ge(t_T, 2 * i + b - 1)
                    gather(q_dram, toku, bass.ds(2 * i + b, 1), 0, tin, b, tin_in)
            copies[:] = [0, MT - 1]
            pool.wait_ge(t_T, MT - 2)
            gather(q_dram, toku, slice(MT - 1, MT), 0, tin, 0, tin_in)

            pool.wait_ge(y_store[0], 16 * (MT // 2 + 1))
            pool.wait_ge(y_store[1], 16 * (MT // 2))
            pool.wait_ge(t_T, MT)
            copies[:] = [0, MT]
            for b in range(2):
                for n, (to, landed) in enumerate(((gring, ga_in), (tin, gb_in))):
                    gather(y_dram, slotu[:, n, :], slice(b, b + 1), n, to, b, landed)
            with pool.Fori(1, NT // 2) as i:
                copies[:] = [0, MT + 4 * i]
                for b in range(2):
                    pool.wait_ge(x1_hi, 2 * i + b - 1)
                    for n, (to, landed) in enumerate(((gring, ga_in), (tin, gb_in))):
                        gather(y_dram, slotu[:, n, :], bass.ds(2 * i + b, 1), n, to, b, landed)

        @block.scalar
        def _(act):
            def setup_item(n, b, source_shape, to):
                act.wait_ge(setup_T, n + 1)
                nc.scalar.copy(to, source_shape).then_inc(setup_hi, 1)

            setup_item(0, 0, main[:, 0, 0:KC * CL].rearrange("p (k c) -> p k c", k=KC),
                       w2part(wslots, 0)[:, :, H:HX])
            setup_item(1, 1, main[:, 1, :].rearrange("p (k c) -> p k c", k=KC), ath[:, 0, :, :])
            with act.Fori(0, KC // 2) as i:
                for b in range(2):
                    setup_item(2 * i + b + 2, b, main[:, b, :].rearrange("p (k c) -> p k c", k=KC),
                               w2part(wslots, 0)[:, :, bass.ds(i * 2 * P + b * P, P)])
            act.wait_ge(const_in, 16 * N_CONST)
            act.wait_ge(lora_in, 16 * KC)
            nc.scalar.copy(split[:, 0, 0, :, :], stage[:, 0, :].rearrange("p (k i) -> p k i", k=KC)
                           ).then_inc(split_hi, 1)
            nc.scalar.copy(split[:, 1, 0, :, :], b1c[:, :].unsqueeze(2).broadcast_to((P, KC, P))
                           ).then_inc(split_hi, 1)
            act.wait_ge(prod, 1)
            nc.scalar.copy(bwx[:, 0, 0:H], main[:, 0, :]).then_inc(prod_hi, 1)
            nc.scalar.copy(bwx[:, 0, H:HX], psg[:, 0:CL]).then_inc(prod_hi, 1)
            act.sem_inc(gate_out, 1)
            act.sem_inc(q_free, 2)

            def steps(t, b, landed):
                act.wait_ge(x_in[b], landed)
                nc.scalar.activation(magnitude[:, b, :], xa[:, b, :], ACT.Abs)
                for g in range(G):
                    act.wait_ge(picked, G * t + g + 1)
                    nc.scalar.activation(bucket[g], xa[:, b, :], ACT.Identity, bias=rnd[:, 0:1],
                                         scale=par2[:, 1, g:g + 1]).then_inc(steps_ready, 1)

            def rounded(t):
                for g in range(OWN, G):
                    act.wait_ge(steps_ready, G * t + g + 1)
                    nc.scalar.activation(bucket[g], bucket[g], ACT.Identity, bias=rnd[:, 1:2]
                                         ).then_inc(ints_ready, 1)

            def dequantised(t):
                for g in range(OWN, G):
                    act.wait_ge(clipped, (G - OWN) * t + g - OWN + 1)
                    nc.scalar.activation(bucket[g], bucket[g], ACT.Copy, scale=par[:, 1, g:g + 1]
                                         ).then_inc(scaled, 1)

            def take(t):
                act.wait_ge(q_T, t + 1)
                nc.scalar.copy(qT[:, :, :], pst[:, :, :]).then_inc(q_Tout, 1)

            def logits(t):
                act.wait_ge(gate, t + 1)
                nc.scalar.copy(rbuf[:, 0, bass.ds(t, 1), :],
                               psl[:, 0:E].unsqueeze(1)).then_inc(gate_out, 1)

            def release(b, stored):
                act.wait_ge(q_store[b], stored)
                act.sem_inc(q_free, 1)

            def weights(j, b):
                act.wait_ge(prod, j + 1)
                nc.scalar.copy(split[:, b, 0, :, :],
                               stage[:, 1 - b, :].rearrange("p (k i) -> p k i", k=KC)
                               ).then_inc(split_hi, 1)

            def merged(j, b):
                act.wait_ge(prod, j + 3)
                act.wait_ge(m_free, j + 1)
                nc.scalar.copy(mev[:, 0, 0:H], main[:, b, :]).then_inc(prod_hi, 1)
                nc.scalar.copy(mev[:, 0, H:HX], psg[:, b * CL:(b + 1) * CL]).then_inc(prod_hi, 1)

            act.wait_ge(consts, 1)

            def turn(i, first):
                for b in range(2):
                    j = 2 * i + b
                    act.wait_ge(w1_in[1 - b], 16 * i + 16)
                    weights(j, b)
                    for c in range(2):
                        t = 2 * j + c
                        steps(t, c, 32 * i + 16 * b + 16)
                        if not (first and b == 0):
                            logits(t - 2)
                        rounded(t)
                        dequantised(t)
                        if not (first and b == 0 and c == 0):
                            take(t - 1)
                            release(1 - c, 32 * i + 16 * b + 16 * c)
                        if not c:
                            merged(j, b)

            turn(0, True)
            with act.Fori(1, KC // 2) as i:
                turn(i, False)
            logits(NT - 2)
            take(NT - 1)
            logits(NT - 1)

            act.wait_ge(prod, KC + 2)
            for c in range(KC):
                act.wait_ge(stage_in[c % RING], STAGED[c % RING] + 16 * (c // RING + 1))
                nc.scalar.copy(expart(wslots, 0, 0)[:, c, :], stage[:, c % RING, :]).then_inc(zero_hi, 1)
            act.wait_ge(exp_in, 1)
            nc.scalar.activation(rcol[:, 3, :], rcol[:, 2, :], ACT.Exp).then_inc(exp_out, 1)

            def take(s, b):
                act.wait_ge(t_T, s + 1)
                if not (isinstance(s, int) and s == 0):
                    act.wait_ge(tile_done, s)
                nc.scalar.copy(split[:, b, 0, :, :], pst[:, :, :]).then_inc(t_hi, 1)
                act.wait_ge(t_rest, s + 1)
                nc.scalar.copy(split[:, b, 1, :, :], pst[:, :, :]).then_inc(t_lo, 1)

            def give(i, s, b):
                act.wait_ge(tile_done, s + 2)
                if not (isinstance(i, int) and i == 0):
                    act.wait_ge(y_store[b], 16 * i)
                nc.scalar.copy(yout[:, b, :], main[:, b, :]).then_inc(y_out, 1)
                act.wait_ge(y_out, s + 3)
                act.dma_start(y_dram[rows(s), :], yout[:, b, :]).then_inc(y_store[b], 16)

            take(0, 0)

            def turn(i):
                take(2 * i + 1, 1)
                give(i, 2 * i, 0)
                take(2 * i + 2, 0)
                give(i, 2 * i + 1, 1)

            turn(0)
            with act.Fori(1, MT // 2) as i:
                turn(i)
            give(MT // 2, MT - 1, 0)

            def exps(i):
                for b in range(2):
                    act.wait_ge(nb_ready, i + 2)
                    nc.scalar.activation(el[:, b, :], zl[:, b, :], ACT.Exp, bias=smx[:, 1, b:b + 1],
                                         scale=1.0 / TEMPERATURE, accum_out=smx[:, 2, b:b + 1]
                                         ).then_inc(soft_done, 1)

            def high(t, b):
                act.wait_ge(x1_ready, t + 3)
                nc.scalar.copy(tile_of(x1, t), gring[:, b, :]).then_inc(x1_kept, 1)
                act.wait_ge(x1_T, t + 1)
                nc.scalar.copy(split[:, b, 0, :, :], pst[:, :, :]).then_inc(x1_hi, 1)

            def pair(i, more):
                act.wait_ge(low_scaled, i + 1)
                nc.scalar.copy(lowr[:, 0, :], lows[:, :]).then_inc(low_hi, 1)
                if more:
                    high(2 * i + 2, 0)
                act.wait_ge(scoresT, i + 1)
                nc.scalar.copy(scT[:, :], psg[:, 0:2 * P]).then_inc(scT_out, 1)
                if more:
                    high(2 * i + 3, 1)
                exps(i)

            high(0, 0)
            high(1, 1)
            with act.Fori(0, NT // 2 - 1) as i:
                pair(i, True)
            pair(NT // 2 - 1, False)

        @block.vector
        def _(dve):
            V = nc.vector
            chain = Chain(dve, dve_chain)
            dve.sem_inc(tile_done, 1)
            dve.sem_inc(y_out, 2)
            dve.sem_inc(exp_lo, 1)
            dve.sem_inc(x1_ready, 2)
            dve.sem_inc(dense_out, 2)
            dve.sem_inc(nb_ready, 1)
            dve.sem_inc(picked, G)
            dve.wait_ge(const_in, 16 * N_CONST)
            dve.wait_ge(iota_done, 11)
            V.max(par2[:, 0, :], par[:, 0, :])
            V.reciprocal(par2[:, 1, :], par[:, 1, :])
            V.tensor_scalar(par2[:, 2, :], par[:, 2, :], -1.0, None, ALU.mult)
            V.tensor_scalar(par2[:, 3, :], par[:, 2, :], -1.0, LEVELS - 1.0, ALU.mult, ALU.add)
            V.memset(zero[:, :], 0.0)
            V.memset(rnd[:, 0:1], ROUND)
            V.memset(rnd[:, 1:2], -ROUND)
            V.memset(ones[:, :], 1.0)
            V.tensor_scalar(negi[:, :], ident[:, :], -1.0, None, ALU.mult)
            V.memset(cacc[:, :], 0.0)
            V.memset(freeat[:, 0:2], 1)
            V.tensor_scalar(tri[:, :], rowi[:, :], parti[:, :], None, ALU.is_gt)
            chain(V.tensor_copy(gring[0:CL, 1, :], gring[0:CL, 0, :].bitcast(I32)))
            V.tensor_scalar(pickT[:, :], gring[0:CL, 1, :], parti[0:CL, :], None, ALU.is_equal)
            chain(V.tensor_tensor(sc[:, 0, :], sc[:, 7, :], par[:, 3, :], ALU.mult))
            chain(V.tensor_reduce(sc[:, 1, 0:1], sc[:, 0, :], axis=AX.X, op=ALU.add))
            chain(V.tensor_tensor(sc[:, 2, :], sc[:, 7, :], sc[:, 5, :], ALU.mult))
            chain(V.tensor_reduce(sc[:, 1, 1:2], sc[:, 2, :], axis=AX.X, op=ALU.add))
            chain(V.tensor_copy(adpf[:, :], adp[:, :]))
            V.tensor_scalar(comb[:, :], adpf[:, :], sc[:, 1, 1:2], sc[:, 1, 0:1], ALU.is_equal,
                            ALU.mult).then_inc(consts, 1)

            def setup_item(n, source, hi, to):
                dve.wait_ge(setup_hi, n + 1)
                V.tensor_tensor(to, source, hi, ALU.subtract).then_inc(setup_lo, 1)

            setup_item(0, main[:, 0, 0:KC * CL].rearrange("p (k c) -> p k c", k=KC),
                       w2part(wf, 0)[:, :, H:HX], w2part(wslots, 1)[:, :, H:HX])
            setup_item(1, main[:, 1, :].rearrange("p (k c) -> p k c", k=KC), athf[:, 0, :, :],
                       ath[:, 1, :, :])
            with dve.Fori(0, KC // 2) as i:
                for b in range(2):
                    at = bass.ds(i * 2 * P + b * P, P)
                    setup_item(2 * i + b + 2, main[:, b, :].rearrange("p (k c) -> p k c", k=KC),
                               w2part(wf, 0)[:, :, at], w2part(wslots, 1)[:, :, at])
            dve.wait_ge(split_hi, 1)
            V.tensor_tensor(split[:, 0, 1, :, :], stage[:, 0, :].rearrange("p (k i) -> p k i", k=KC),
                            splitf[:, 0, 0, :, :], ALU.subtract).then_inc(split_lo, 1)
            dve.wait_ge(split_hi, 2)
            V.tensor_tensor(split[:, 1, 1, :, :], b1c[:, :].unsqueeze(2).broadcast_to((P, KC, P)),
                            splitf[:, 1, 0, :, :], ALU.subtract).then_inc(split_lo, 1)
            dve.wait_ge(prod_hi, 2)
            V.tensor_tensor(bwx[:, 1, 0:H], main[:, 0, :], bwxf[:, 0, 0:H], ALU.subtract)
            V.tensor_tensor(bwx[:, 1, H:HX], psg[:, 0:CL], bwxf[:, 0, H:HX], ALU.subtract).then_inc(prod_lo, 1)
            dve.wait_ge(prod, 2)
            V.tensor_tensor(biasx[:, 0:H], main[:, 1, :], biasx[:, 0:H], ALU.add)
            V.tensor_copy(biasx[:, H:HX], psg[:, CL:2 * CL]).then_inc(prod_lo, 1)

            def quantise(t, b):
                def low(g):
                    return par2[:, 2, g:g + 1]

                def high(g):
                    return par2[:, 3, g:g + 1]

                def below(g):
                    V.tensor_scalar(mask[:, g % 4, :], magnitude[:, b, :], par2[:, 0, g - 1:g], None, ALU.is_le)

                def pick(g):
                    dve.wait_ge(picked, G * t + G + g)
                    if OWN <= g < G:
                        dve.wait_ge(scaled, (G - OWN) * t + g - OWN + 1)
                    dve.sem_inc(pick_seen, 1)
                    V.copy_predicated(qrow[:, b, :], mask[:, g % 4, :],
                                      bucket[g] if g < G else zero[:, :].broadcast_to((P, H))
                                      ).then_inc(picked if g < G else q_ready, 1)

                def finish(g, to):
                    return V.tensor_scalar(to, bucket[g], high(g), par[:, 1, g:g + 1], ALU.min, ALU.mult)

                for g in range(OWN):
                    dve.wait_ge(steps_ready, G * t + g + 1)
                    last = V.tensor_scalar(bucket[g], bucket[g], ROUND, low(g), ALU.subtract, ALU.max)
                last.then_inc(lower_done, 1)
                below(1)
                dve.wait_ge(lower_done, t + 1)
                finish(1, bucket[1])
                finish(2, bucket[2])
                below(2)
                dve.wait_ge(q_free, t + 1)
                finish(0, qrow[:, b, :]).then_inc(picked, 1)
                below(3)
                pick(1)
                below(4)
                pick(2)
                for g in range(OWN, G):
                    dve.wait_ge(ints_ready, (G - OWN) * t + g - OWN + 1)
                    V.tensor_scalar(bucket[g], bucket[g], low(g), high(g), ALU.max, ALU.min).then_inc(clipped, 1)
                    if g == OWN:
                        below(5)
                for g in range(OWN, G + 1):
                    pick(g)
                    if g + 3 <= G:
                        below(g + 3)

            with dve.Fori(0, KC // 2) as i:
                for b in range(2):
                    j = 2 * i + b

                    dve.wait_ge(split_hi, j + 3)
                    V.tensor_tensor(split[:, b, 1, :, :], stage[:, 1 - b, :].rearrange("p (k i) -> p k i", k=KC),
                                    splitf[:, b, 0, :, :], ALU.subtract).then_inc(split_lo, 1)
                    quantise(4 * i + 2 * b, 0)
                    dve.wait_ge(prod_hi, 2 * j + 4)
                    V.tensor_tensor(mev[:, 1, 0:H], main[:, b, :], mevf[:, 0, 0:H], ALU.subtract)
                    V.tensor_tensor(mev[:, 1, H:HX], psg[:, b * CL:(b + 1) * CL], mevf[:, 0, H:HX],
                                    ALU.subtract).then_inc(prod_lo, 1)
                    quantise(4 * i + 2 * b + 1, 1)

            dve.wait_ge(gate_out, NT + 1)

            def best(logits, hot, top):
                wide = rcol[:, top, :].unsqueeze(2).broadcast_to((P, NT, E))
                chain(V.tensor_reduce(rcol[:, top, :], logits, axis=AX.X, op=ALU.max))
                chain(V.tensor_tensor(rbuf[:, 1, :, :], logits, wide, ALU.is_equal))
                chain(V.tensor_tensor(rbuf[:, 1, :, :], rbuf[:, 1, :, :],
                                      sc[:, 6:7, :].broadcast_to((P, NT, E)), ALU.mult))
                chain(V.tensor_reduce(rcol[:, 4, :], rbuf[:, 1, :, :], axis=AX.X, op=ALU.max))
                chain(V.tensor_tensor(hot, rbuf[:, 1, :, :],
                                      rcol[:, 4, :].unsqueeze(2).broadcast_to((P, NT, E)), ALU.is_equal))

            best(rbuf[:, 0, :, :], rbuf[:, 2, :, :], 0)
            chain(V.scalar_tensor_tensor(rbuf[:, 4, :, :], rbuf[:, 2, :, :], -3.0e38, rbuf[:, 0, :, :],
                                         ALU.mult, ALU.add))
            best(rbuf[:, 4, :, :], rbuf[:, 3, :, :], 1)
            V.tensor_tensor(rcol[:, 2, :], rcol[:, 1, :], rcol[:, 0, :], ALU.subtract).then_inc(exp_in, 1)
            V.tensor_tensor(hotB[:, 0, :].rearrange("p (t e) -> p t e", e=E), rbuf[:, 2, :, :],
                            rbuf[:, 3, :, :], ALU.add).then_inc(hots_ready, 1)
            dve.wait_ge(exp_out, 1)
            chain(V.tensor_scalar(rcol[:, 5, :], rcol[:, 3, :], 1.0, None, ALU.add))
            chain(V.reciprocal(wts[:, 0, :], rcol[:, 5, :]))
            V.tensor_tensor(wts[:, 1, :], rcol[:, 3, :], wts[:, 0, :], ALU.mult)

            def scan(a, b, n, at):
                shift = 1
                while shift < n:
                    V.tensor_copy(at(b, 0, shift), at(a, 0, shift))
                    chain(V.tensor_tensor(at(b, shift, n), at(a, shift, n), at(a, 0, n - shift), ALU.add))
                    a, b, shift = b, a, 2 * shift
                return a

            dve.wait_ge(counted, 1)
            chain(V.tensor_copy(rbuf[:, 5, :, :], psg[:, 0:P].rearrange("p (t e) -> p t e", e=E)))
            chain(V.tensor_copy(rbuf[:, 6, :, :], rbuf[:, 5, :, :]))
            s = scan(6, 7, NT, lambda buf, lo, hi: rbuf[:, buf, lo:hi, :])
            chain(V.tensor_tensor(rbuf[:, 8, :, :], rbuf[:, s, :, :], rbuf[:, 5, :, :], ALU.subtract))
            chain(V.tensor_tensor(rbuf[:, 8, :, :], rbuf[:, 8, :, :],
                                  psl[:, 0:P].rearrange("p (t e) -> p t e", e=E), ALU.add))
            chain(V.tensor_scalar(tint[:, :], rbuf[:, s, NT - 1, :], P - 1.0, None, ALU.add))
            chain(V.tensor_scalar(tint[:, :], tint[:, :], 7, None, ALU.logical_shift_right))
            chain(V.tensor_copy(sc[:, 0, :], tint[:, :]))
            chain(V.tensor_copy(sc[:, 1, :], sc[:, 0, :]))
            s = scan(1, 2, E, lambda buf, lo, hi: sc[:, buf, lo:hi])
            ends = sc[:, s, :]
            chain(V.tensor_tensor(sc[:, 3, :], ends, sc[:, 0, :], ALU.subtract))
            chain(V.scalar_tensor_tensor(rbuf[:, 9, :, :], sc[:, 3:4, :].broadcast_to((P, NT, E)), float(P),
                                         rbuf[:, 8, :, :], ALU.mult, ALU.add))
            for n in range(2):
                chain(V.tensor_tensor(rbuf[:, 4 + n, :, :], rbuf[:, 9, :, :], rbuf[:, 2 + n, :, :], ALU.mult))
                chain(V.tensor_reduce(slots[:, n, :], rbuf[:, 4 + n, :, :], axis=AX.X, op=ALU.add))
            V.tensor_copy(slotu[:, :, :], slots[:, :, :])
            chain(V.tensor_copy(sli[:, :, :], slots[:, :, :]))
            chain(V.tensor_scalar(sli2[:, 0, :, :], sli[:, :, :], 7, None, ALU.logical_shift_right))
            chain(V.tensor_scalar(sli2[:, 1, :, :], sli[:, :, :], P - 1, None, ALU.bitwise_and))
            V.tensor_copy(shi[:, :, :], sli2[:, 0, :, :])
            chain(V.tensor_copy(slo[:, :, :], sli2[:, 1, :, :]))
            n2 = 2 * NT
            flat = lambda a: a.rearrange("p n t -> p (n t)")
            V.tensor_tensor(hotB[:, :, :], rowi[:, :].unsqueeze(1).broadcast_to((P, n2, P)),
                            flat(slo[:, :, :]).unsqueeze(2).broadcast_to((P, n2, P)), ALU.is_equal)
            chain(V.tensor_tensor(hotA[:, :, :], mt_row[:, :].unsqueeze(1).broadcast_to((P, n2, MT)),
                                  flat(shi[:, :, :]).unsqueeze(2).broadcast_to((P, n2, MT)), ALU.is_equal))
            V.tensor_scalar(hotX[:, :, 0:MT], hotA[:, :, :], parti[:, :], None, ALU.mult)
            V.tensor_tensor(hotX[:, :, MT:2 * MT], hotA[:, :, :],
                            flat(tcol[:, :, :]).unsqueeze(2).broadcast_to((P, n2, MT)),
                            ALU.mult).then_inc(slots_ready, 1)
            chain(V.tensor_tensor(mt_cmp[:, :, :], mt_row[:, :].unsqueeze(2).broadcast_to((P, MT, E - 1)),
                                  ends[:, 0:E - 1].unsqueeze(1).broadcast_to((P, MT, E - 1)), ALU.is_ge))
            chain(V.tensor_reduce(mt_exp[:, :], mt_cmp[:, :, :], axis=AX.X, op=ALU.add))
            V.tensor_scalar(mt_need[:, :], mt_exp[:, :], float(KC), 1.0, ALU.mult, ALU.add)
            V.tensor_scalar(freeat[:, 2:E + 1], ends[:, 0:E - 1], 1.0, None, ALU.add)
            chain(V.tensor_copy(mt_int[:, :], mt_exp[:, :]))
            chain(V.tensor_scalar(mt_int[:, :], mt_int[:, :], 1, None, ALU.bitwise_and))
            chain(V.tensor_copy(mt_exp[:, :], mt_int[:, :]))
            chain(V.tensor_scalar(mt_par[:, :], mt_exp[:, :], float(SLOT1), None, ALU.mult))
            dve.wait_ge(placed, 1)
            chain(V.tensor_copy(mt_cmp[:, :, 0], psg[:, 0:MT]))
            V.scalar_tensor_tensor(toku[:, :], psg[:, MT:2 * MT], float(P), mt_cmp[:, :, 0], ALU.mult,
                                   ALU.add).then_inc(routed, 1)

            def expert(e, odd):
                for c in range(KC):
                    dve.wait_ge(stage_in[c % RING], STAGED[c % RING] + 16 * (c // RING + 1) + e * 32)
                    V.tensor_copy(expart(wslots, odd, 0)[:, c, :], stage[:, c % RING, :]).then_inc(exp_hi, 1)
                    dve.wait_ge(exp_hi, (e - 1) * KC + c + 1)
                    V.tensor_tensor(expart(wslots, odd, 1)[:, c, :], stage[:, c % RING, :],
                                    expart(wf, odd, 0)[:, c, :], ALU.subtract).then_inc(exp_lo, 1)

            dve.wait_ge(m_store, 16 * KC)
            for b in range(2):
                dve.wait_ge(q_store[b], 16 * NT // 2)
            expert(1, 1)
            with dve.Fori(1, E // 2) as pair:
                for odd in range(2):
                    need = dve.value_load(freeat[0:1, bass.ds(2 * pair + odd, 1)], min_val=1, max_val=MT + 1)
                    dve.wait_ge(tile_done, need)
                    expert(2 * pair + odd, odd)

            dve.wait_ge(y_store[0], 16 * (MT // 2 + 1))
            dve.wait_ge(y_store[1], 16 * (MT // 2))

            def total(i, b, t):
                dve.wait_ge(xc_in[b], 16 * i + 16)
                dve.wait_ge(ga_in[b], 16 * i + 16)
                dve.wait_ge(gb_in[b], 16 * i + 16)
                at = (lambda n: wts[:, n, t:t + 1]) if isinstance(t, int) else (
                    lambda n: wts[:, n, bass.ds(t, 1)])
                chain(V.scalar_tensor_tensor(gring[:, b, :], gring[:, b, :], at(0), stage[:, b, :],
                                             ALU.mult, ALU.add))
                V.scalar_tensor_tensor(gring[:, b, :], tin[:, b, :], at(1), gring[:, b, :],
                                       ALU.mult, ALU.add).then_inc(x1_ready, 1)

            def low(t, b):
                dve.wait_ge(x1_hi, t + 1)
                V.tensor_tensor(split[:, b, 1, :, :], pst[:, :, :], splitf[:, b, 0, :, :],
                                ALU.subtract).then_inc(x1_lo, 1)

            def scale(i):
                dve.wait_ge(low_done, i + 1)
                V.tensor_scalar(lows[:, :], psl[:, 0:2 * P], comb[:, bass.ds(i, 1)], None,
                                ALU.mult).then_inc(low_scaled, 1)
                dve.wait_ge(low_hi, i + 1)
                V.tensor_tensor(lowr[:, 1, :], lows[:, :], lowrf[:, 0, :], ALU.subtract).then_inc(low_lo, 1)

            def result(t, b):
                dve.wait_ge(layer_done, t + 1)
                V.tensor_tensor(stage[:, 2 + b, :], main[:, b, :], biasx[:, 0:H],
                                ALU.add).then_inc(dense_out, 1)

            def add(i, t, b):
                if not (isinstance(i, int) and i == 0):
                    dve.wait_ge(out_store[b], 16 * i)
                dve.wait_ge(x1_kept, t + 1)
                V.scalar_tensor_tensor(yout[:, b, :], stage[:, 2 + b, :], qsel[:, bass.ds(t, 1)],
                                       tile_of(x1, t), ALU.mult, ALU.add).then_inc(out_ready, 1)

            def judge(i):
                dve.wait_ge(scores, i + 1)
                chain(V.tensor_tensor(zl[:, :, :], psl[:, 2 * P:4 * P].rearrange("p (b c) -> p b c", b=2)[:, :, CL:P],
                                      biasx[:, H:HX].unsqueeze(1).broadcast_to((P, 2, CL)), ALU.add))
                chain(V.tensor_reduce(smx[:, 0, :], zl[:, :, :], axis=AX.X, op=ALU.max))
                V.tensor_scalar(smx[:, 1, :], smx[:, 0, :], -1.0 / TEMPERATURE, None, ALU.mult).then_inc(nb_ready, 1)
                dve.wait_ge(soft_done, 2 * i + 2)
                chain(V.reciprocal(smx[:, 3, :], smx[:, 2, :]))
                for b in range(2):
                    last = V.tensor_scalar(hits[:, b, :], el[:, b, :], smx[:, 3, b:b + 1], THRESHOLD,
                                           ALU.mult, ALU.is_gt)
                chain(last)
                V.tensor_reduce(qsel[:, bass.ds(2 * i, 2)], hits[:, :, :], axis=AX.X, op=ALU.max)
                for b in range(2):
                    chain(V.tensor_tensor(cacc[:, :], cacc[:, :], hits[:, b, :], ALU.max))

            def whole(i, more):
                scale(i)
                if more:
                    total(i + 1, 0, 2 * i + 2)
                    low(2 * i + 2, 0)
                    total(i + 1, 1, 2 * i + 3)
                result(2 * i, 0)
                result(2 * i + 1, 1)
                if more:
                    low(2 * i + 3, 1)
                judge(i)
                if more:
                    add(i, 2 * i, 0)
                    add(i, 2 * i + 1, 1)

            total(0, 0, 0)
            total(0, 1, 1)
            low(0, 0)
            low(1, 1)
            chain.turn(0, chain.here(), 0)
            whole(0, True)
            first, per = chain.here(), 8
            with dve.Fori(1, NT // 2 - 1) as i:
                chain.turn(i - 1, first, per)
                whole(i, True)
                assert chain.n == per, chain.n
            chain.turn(0, first + per * (NT // 2 - 2), 0)
            whole(NT // 2 - 1, False)

            V.tensor_copy(caccb[:, :], cacc[:, :]).then_inc(cacc_ready, 1)
            for b in range(2):
                add(NT // 2 - 1, NT - 2 + b, b)
            dve.wait_ge(clu_done, 1)
            chain(V.tensor_copy(clu[:, :], psl[0:CL, 0:1]))
            V.tensor_scalar(cselb[:, :], ones[0:CL, :], clu[:, :], 0.5, ALU.mult, ALU.is_gt
                            ).then_inc(csel_ready, 1)
            dve.wait_ge(rowsel_done, 1)
            chain(V.tensor_reduce(smx[:, 0, 0:1], main[:, 0, :], axis=AX.X, op=ALU.min))
            V.tensor_copy(flag[:, :], smx[:, 0, 0:1]).then_inc(flag_ready, 1)
            dve.wait_ge(flag_ready, 1)
            full = dve.value_load(flag[0:1, 0:1], min_val=0, max_val=1)
            with dve.If(full < 1):
                count = gring[:, 0, :].bitcast(U8)[:, 0:H]
                V.tensor_scalar(count, main[:, 0, :], 0.5, None, ALU.is_gt).then_inc(again_seen, 1)
                dve.wait_ge(again_seen, 1)
                with dve.Fori(0, NT // 2) as i:
                    for b in range(2):
                        dve.wait_ge(again_in[b], 16 * i + 16)
                        dve.wait_ge(again_free, 2 * i + b + 1)
                        V.tensor_copy(tin[:, b, :], tile_of(x1, 2 * i + b)).then_inc(again_seen, 1)
                        dve.wait_ge(again_seen, 4 * i + 2 * b + 2)
                        dve.sem_inc(again_seen, 1)
                        V.copy_predicated(tin[:, b, :], count, yout[:, b, :]).then_inc(again_ready, 1)

        @block.tensor
        def _(pe):
            def mm(o, l, r, start, stop):
                return nc.tensor.matmul(o, l, r, start=start, stop=stop)

            def three(cols, stationary, moving):
                for k in range(KC):
                    for sp_, mp in ((0, 0), (0, 1), (1, 0)):
                        for o, lo, hi in cols:
                            last = mm(o, stationary(k, sp_), moving(k, mp, lo, hi),
                                      k == 0 and (sp_, mp) == (0, 0), k == KC - 1 and (sp_, mp) == (1, 0))
                return last

            pe.wait_ge(iota_done, 2)
            pe.wait_ge(stage_in[0], 16)
            for k in range(KC):
                last = nc.tensor.transpose(main[:, 0, k * CL:(k + 1) * CL], stage[0:CL, 0, k * P:(k + 1) * P],
                                           ident[0:CL, 0:CL])
            last.then_inc(setup_T, 1)
            pe.wait_ge(stage_in[1], 16)
            for k in range(KC):
                last = nc.tensor.transpose(main[:, 1, k * P:(k + 1) * P], stage[:, 1, k * P:(k + 1) * P],
                                           ident[:, :])
            last.then_inc(setup_T, 1)
            with pe.Fori(0, KC // 2) as i:
                for b in range(2):
                    pe.wait_ge(stage_in[b], 16 * i + 32)
                    pe.wait_ge(setup_lo, 2 * i + b + 1)
                    for k in range(KC):
                        last = nc.tensor.transpose(main[:, b, k * P:(k + 1) * P],
                                                   stage[:, b, k * P:(k + 1) * P], ident[:, :])
                    last.then_inc(setup_T, 1)
            pe.wait_ge(setup_lo, KC + 2)

            def product(m, b):
                pe.wait_ge(split_lo, m + 1)
                last = three([(main[:, b, 0:NB], 0, NB), (main[:, b, NB:H], NB, H),
                              (psg[:, b * CL:(b + 1) * CL], H, HX)],
                             lambda k, part: split[:, b, part, k, :],
                             lambda k, part, lo, hi: w2part(wslots, part)[:, k, lo:hi])
                last.then_inc(prod, 1)

            product(0, 0)
            pe.wait_ge(prod_lo, 1)
            product(1, 1)
            pe.wait_ge(consts, 1)

            def turn_q(t, b):
                pe.wait_ge(q_ready, t + 1)
                for k in range(KC):
                    last = nc.tensor.transpose(pst[:, k, :], qrow[:, b, k * P:(k + 1) * P], ident[:, :])
                last.then_inc(q_T, 1)

            def gating(t):
                pe.wait_ge(q_Tout, t + 1)
                pe.wait_ge(gate_out, t + 1)
                for k in range(KC):
                    last = mm(psl[:, 0:E], qT[:, k, :], gw[:, k, :], k == 0, k == KC - 1)
                last.then_inc(gate, 1)

            def turn(i, first):
                for b in range(2):
                    t = 4 * i + 2 * b
                    before = not (first and b == 0)
                    if before:
                        turn_q(t - 1, 1)
                    pe.wait_ge(prod_lo, 2 * i + b + 2)
                    product(2 * i + b + 2, b)
                    if before:
                        gating(t - 1)
                    turn_q(t, 0)
                    gating(t)

            turn(0, True)
            with pe.Fori(1, KC // 2) as i:
                turn(i, False)
            turn_q(NT - 1, 1)
            gating(NT - 1)

            pe.wait_ge(prod_lo, KC + 2)
            pe.wait_ge(gate_out, NT + 1)
            pe.wait_ge(hots_ready, 1)
            mm(psl[:, 0:P], tri[:, :], hotB[:, 0, :], True, True)
            mm(psg[:, 0:P], ones[:, :], hotB[:, 0, :], True, True).then_inc(counted, 1)
            pe.wait_ge(slots_ready, 1)
            for n in range(2 * NT):
                last = mm(psg[:, 0:2 * MT], hotB[:, n, :], hotX[:, n, :], n == 0, n == 2 * NT - 1)
            last.then_inc(placed, 1)
            pe.wait_ge(routed, 1)

            def turn_rows(nth, s, b):
                pe.wait_ge(tin_in[b], 16 * nth)
                for k in range(KC):
                    last = nc.tensor.matmul(pst[:, k, :], tin[:, b, k * P:(k + 1) * P], ident[:, :],
                                            start=k % 4 == 0, stop=False, is_transpose=True,
                                            skip_group_check=True)
                last.then_inc(t_T, 1)

            def rest(s, b):
                pe.wait_ge(t_hi, s + 1)
                for h in range(2):
                    last = nc.tensor.matmul(pst[:, 4 * h:4 * h + 4, :], negi[:, :],
                                            split[:, b, 0, 4 * h:4 * h + 4, :],
                                            start=False, stop=True, skip_group_check=True)
                last.then_inc(t_rest, 1)

            def multiply(s, b, ahead, nth):
                if ahead:
                    turn_rows(nth, s + 1, 1 - b)
                at = (lambda tab: tab[0:1, s:s + 1]) if isinstance(s, int) else (
                    lambda tab: tab[0:1, bass.ds(s, 1)])
                need = pe.value_load(at(mt_need), min_val=1, max_val=E * KC)
                base = pe.value_load(at(mt_par), min_val=0, max_val=SLOT1)
                pe.wait_ge(exp_lo, need)
                pe.wait_ge(y_out, s + 1)
                for k in range(KC):
                    if ahead and k == KC // 2:
                        rest(s + 1, 1 - b)
                    for sp_, mp in ((0, 0), (0, 1), (1, 0)):
                        for h in range(2):
                            last = mm(main[:, b, h * NB:(h + 1) * NB], split[:, b, sp_, k, :],
                                      wslots[:, bass.ds(base + mp * WE + k * H + h * NB, NB)],
                                      k == 0 and (sp_, mp) == (0, 0), k == KC - 1 and (sp_, mp) == (1, 0))
                last.then_inc(tile_done, 1)

            turn_rows(1, 0, 0)
            rest(0, 0)
            pe.wait_ge(zero_lo, KC)
            with pe.Fori(0, MT // 2) as i:
                pe.wait_ge(t_lo, 2 * i + 1)
                multiply(2 * i, 0, True, i + 1)
                pe.wait_ge(t_lo, 2 * i + 2)
                multiply(2 * i + 1, 1, True, i + 2)
            pe.wait_ge(t_lo, MT)
            multiply(MT - 1, 0, False, 0)

            def turn_x1(t, b):
                pe.wait_ge(x1_ready, t + 3)
                for k in range(KC):
                    last = nc.tensor.transpose(pst[:, k, :], gring[:, b, k * P:(k + 1) * P], ident[:, :])
                last.then_inc(x1_T, 1)

            def heads(b):
                return [(main[:, b, 0:NB], 0, NB), (main[:, b, NB:H], NB, H)]

            def product1(t, b):
                pe.wait_ge(dense_out, t + 1)
                pe.wait_ge(x1_lo, t + 1)
                for k in range(KC):
                    for sp_, mp in ((0, 0), (0, 1), (1, 0)):
                        for o, lo, hi in heads(b):
                            mm(o, split[:, b, sp_, k, :], w2part(wslots, mp)[:, k, lo:hi],
                               k == 0 and (sp_, mp) == (0, 0), False)

            def lora(b):
                for sp_, mp in ((0, 0), (0, 1), (1, 0)):
                    for o, lo, hi in heads(b):
                        last = mm(o, lowr[:, sp_, b * P:(b + 1) * P], bwx[:, mp, lo:hi], False, (sp_, mp) == (1, 0))
                last.then_inc(layer_done, 1)

            def both(part, k):
                return split[:, :, part, k, :]

            EDGE = slice(HX - P, HX)

            def pair(i, more):
                product1(2 * i, 0)
                pe.wait_ge(x1_lo, 2 * i + 2)
                pe.wait_ge(nb_ready, i + 1)
                last = three([(psl[:, 0:2 * P], 0, 0)], lambda k, part: ath[:, part, k, :],
                             lambda k, part, lo, hi: both(part, k))
                last.then_inc(low_done, 1)
                for k in range(KC):
                    for sp_, mp in ((0, 0), (0, 1), (1, 0)):
                        mm(psg[:, 0:2 * P], w2part(wslots, sp_)[:, k, EDGE], both(mp, k),
                           k == 0 and (sp_, mp) == (0, 0), False)
                if more:
                    turn_x1(2 * i + 2, 0)
                pe.wait_ge(low_lo, i + 1)
                for sp_, mp in ((0, 0), (0, 1), (1, 0)):
                    last = mm(psg[:, 0:2 * P], bwx[:, sp_, EDGE], lowr[:, mp, :], False, (sp_, mp) == (1, 0))
                last.then_inc(scoresT, 1)
                lora(0)
                product1(2 * i + 1, 1)
                lora(1)
                pe.wait_ge(scT_out, i + 1)
                for b in range(2):
                    last = nc.tensor.transpose(psl[:, (2 + b) * P:(3 + b) * P], scT[:, b * P:(b + 1) * P],
                                               ident[:, :])
                last.then_inc(scores, 1)
                if more:
                    turn_x1(2 * i + 3, 1)

            turn_x1(0, 0)
            pe.wait_ge(x1_lo, 1)
            turn_x1(1, 1)
            pe.wait_ge(m_in, 32)
            with pe.Fori(0, NT // 2 - 1) as i:
                pair(i, True)
            pair(NT // 2 - 1, False)

            pe.wait_ge(cacc_ready, 1)
            mm(psl[0:CL, 0:1], caccb[:, :], ones[:, 0:1], True, True).then_inc(clu_done, 1)
            pe.wait_ge(csel_ready, 1)
            mm(main[:, 0, 0:NB], cselb[:, :], pickT[:, 0:NB], True, True)
            mm(main[:, 0, NB:H], cselb[:, :], pickT[:, NB:H], True, True).then_inc(rowsel_done, 1)


_INS = ["x", "condB_thresholds", "condB_deltas", "condB_zeropoints", "itok_B_1_7", "L0_ffn_gate_w",
        "L0_ffn_expert_w", "L1_cond_weight", "L1_cond_bias", "L1_cond_lora_a_weights",
        "L1_cond_lora_b_weights", "L1_cond_scaling_factors", "L1_ffn_weight", "L1_ffn_bias",
        "L1_ffn_centroids", "L1_ffn_assignments"]


def kernel(**inputs):
    import concourse.bacc as bacc
    from concourse.bass_utils import run_bass_kernel_spmd

    nc = bacc.Bacc("TRN2", target_bir_lowering=False, num_devices=1, dynamic_dma_scratch_size=4096)
    arrays, args = {}, []
    for name in _INS:
        a = np.ascontiguousarray(inputs[name])
        if name == "x":
            a = a.reshape(TOK, H)
        arrays[f"in_{name}"] = a
        args.append(nc.dram_tensor(f"in_{name}", a.shape, mybir.dt.from_np(a.dtype), kind="ExternalInput").ap())
    out = nc.dram_tensor("out", [TOK, H], F32, kind="ExternalOutput").ap()
    build(nc, *args, out)
    r = run_bass_kernel_spmd(nc, [arrays], core_ids=[0])
    return r.results[0]["out"].reshape(inputs["x"].shape)
```

```python
from contextlib import ExitStack, nullcontext

import numpy as np

import concourse.bass as bass
from concourse import mybir

F32 = mybir.dt.float32
F32R = mybir.dt.float32r
BF16 = mybir.dt.bfloat16
I32 = mybir.dt.int32
U32 = mybir.dt.uint32
U8 = mybir.dt.uint8
ALU = mybir.AluOpType
ACT = mybir.ActivationFunctionType
AX = mybir.AxisListType

P = 128
H = 1024
KC = H // P
TOK = 2048
NT = TOK // P
E = 8
TOPK = 2
G = 8
LEVELS = 64
OWN = 3
RING = 4
CL = 64
HX = H + CL
R = 16
LOW = slice(CL, CL + R)
A = 8
FULL = TOK * TOPK // P
MT = FULL + E - 1
NB = 512
W2X = KC * HX
WE = KC * H
SLOT1 = 2 * W2X
ROUND = 1.5 * 2.0 ** 23
TEMPERATURE = 0.1
THRESHOLD = 0.01


class Chain:

    def __init__(self, engine, sem):
        self.engine, self.sem, self.base, self.n = engine, sem, 0, 0

    def __call__(self, instruction):
        self.n += 1
        instruction.then_inc(self.sem, 1)
        self.engine.wait_ge(self.sem, self.base + self.n)

    def turn(self, i, first, per):
        self.base, self.n = first + i * per, 0

    def here(self):
        return self.base + self.n


def build(nc, x, thresholds, deltas, zero_points, adapter, gate_w, expert_w, w1, b1, lora_a, lora_b,
          scaling, w2, b2, centroids, assignments, out):
    def scratch(name, shape, dt):
        return nc.dram_tensor(name, shape, dt).ap()

    q_dram = scratch("q_dram", [TOK, H], F32)
    y_dram = scratch("y_dram", [MT * P, H], F32)
    b_dram = scratch("b_dram", [P, 2, HX], F32)
    m_dram = scratch("m_dram", [P, KC, HX], F32)

    with ExitStack() as ctx:
        def sb(name, shape, dt=F32):
            return ctx.enter_context(nc.sbuf_tensor(name, shape, dt))

        def sem(name):
            return ctx.enter_context(nc.semaphore(name))

        with ExitStack() as under:
            def over(name, shape, dt=F32):
                return under.enter_context(nc.sbuf_tensor(name, shape, dt))
            over("under_slot0", [P, SLOT1])
            mev = over("mev", [P, 2, HX])
            qrow = over("qrow", [P, 2, H])
            qT = over("qT", [P, KC, P])
            rbuf = over("rbuf", [P, 10, NT, E])
            mt_cmp = over("mt_cmp", [P, MT, E - 1])
            rowi = over("rowi", [P, P], BF16)
            tri = over("tri", [P, P], BF16)
            adpf = over("adpf", [P, E])
            b1c = over("b1c", [P, KC])
            gw = over("gw", [P, KC, E])
            par = over("par", [P, 4, G])
            par2 = over("par2", [P, 4, G])
            rnd = over("rnd", [P, 2])
            sc = over("sc", [P, 8, E])
            rcol = over("rcol", [P, 8, NT])
            slots = over("slots", [P, 2, NT])
            sli = over("sli", [P, 2, NT], I32)
            sli2 = over("sli2", [P, 2, 2, NT], I32)
            slo = over("slo", [P, 2, NT], BF16)
            shi = over("shi", [P, 2, NT], BF16)
            tcol = over("tcol", [P, 2, NT], BF16)
            mt_row = over("mt_row", [P, MT], BF16)
            mt_exp = over("mt_exp", [P, MT])
            mt_int = over("mt_int", [P, MT], I32)
            tint = over("tint", [P, E], I32)
            with ExitStack() as inner:
                def first(name, shape, dt=F32):
                    return inner.enter_context(nc.sbuf_tensor(name, shape, dt))
                xa = first("xa", [P, 2, H])
                some = first("some", [P, 4, H])
                mask = first("mask", [P, 4, H], U8)
            hotB = over("hotB", [P, 2 * NT, P], BF16)
            hotA = over("hotA", [P, 2 * NT, MT], BF16)
            hotX = over("hotX", [P, 2 * NT, 2 * MT], BF16)
        with ExitStack() as under:
            under.enter_context(nc.sbuf_tensor("under_slot0b", [P, SLOT1], F32))
            x1 = under.enter_context(nc.sbuf_tensor("x1", [P, NT, H], F32))
        wslots = sb("wslots", [P, 2 * W2X + 2 * WE], F32R)
        ath = sb("ath", [P, 2, KC, P], F32R)
        bwx = sb("bwx", [P, 2, HX], F32R)
        split = sb("split", [P, 2, 2, KC, P], F32R)
        stage = sb("stage", [P, RING, H])
        gring = sb("gring", [P, 2, H])
        tin = sb("tin", [P, 2, H])
        yout = sb("yout", [P, 2, H])
        biasx = sb("biasx", [P, HX])
        pickT = sb("pickT", [CL, H], BF16)
        ident = sb("ident", [P, P])
        parti = sb("parti", [P, 1])
        ones = sb("ones", [P, P], BF16)
        adp = sb("adp", [P, E], I32)
        comb = sb("comb", [P, E])
        wts = sb("wts", [P, 2, NT])
        idx = sb("idx", [P, 2, 2], U32)
        slotu = sb("slotu", [P, 2, NT], U32)
        mt_par = sb("mt_par", [P, MT], I32)
        mt_need = sb("mt_need", [P, MT], I32)
        freeat = sb("freeat", [P, E + 1], I32)
        toku = sb("toku", [P, MT], U32)
        lowr = sb("lowr", [P, 2, 2 * P], F32R)
        spare = stage[:, 2, :]
        zl, el, hits = (spare[:, n * 2 * CL:(n + 1) * 2 * CL].rearrange("p (b c) -> p b c", b=2) for n in range(3))
        cacc = spare[:, 6 * CL:7 * CL]
        cselb = spare[0:CL, 7 * CL:8 * CL].bitcast(BF16)
        scT = spare[:, 8 * CL:12 * CL]
        lows = scT[LOW, :]
        heads_w = sb("heads_w", [P, 2, KC, CL + R], F32R)
        caccb = sb("caccb", [P, CL], BF16)
        smx = sb("smx", [P, 4, 2])
        qsel = sb("qsel", [P, NT])
        clu = sb("clu", [CL, 1])
        used = sb("used", [P, 1], I32)
        stored = sb("stored", [P, 2], I32)
        flag = sb("flag", [P, 1], I32)

        wf = wslots[:, :].bitcast(F32)
        splitf = split[:, :, :, :, :].bitcast(F32)
        athf = ath[:, :, :, :].bitcast(F32)
        bwxf = bwx[:, :, :].bitcast(F32)
        lowrf = lowr[:, :, :].bitcast(F32)

        bucket = [some[:, n, :] for n in range(4)] + [buf[:, n, :] for buf in (tin, yout) for n in range(2)]
        magnitude = stage[:, 2:4, :]

        def by(row, g):
            return row[:, G - 1 - g:G - g]

        def w2part(tensor, part):
            return tensor[:, part * W2X:(part + 1) * W2X].rearrange("p (k n) -> p k n", k=KC)

        def expart(tensor, odd, part):
            o = odd * SLOT1 + part * WE
            return tensor[:, o:o + WE].rearrange("p (k n) -> p k n", k=KC)

        main = ctx.enter_context(nc.psum_tensor("main", [P, 2, H], F32))
        pst = ctx.enter_context(nc.psum_tensor("pst", [P, KC, P], F32))
        psg = ctx.enter_context(nc.psum_tensor("psg", [P, NB], F32))
        psl = ctx.enter_context(nc.psum_tensor("psl", [P, NB], F32))

        const_in = sem("const_in")
        iota_done = sem("iota_done")
        par_in = sem("par_in")
        steps_known = sem("steps_known")
        consts = sem("consts")
        lora_in = sem("lora_in")
        stage_in = [sem(f"stage_in{i}") for i in range(4)]
        w1_in = [sem(f"w1_in{i}") for i in range(2)]
        setup_T = sem("setup_T")
        setup_hi = sem("setup_hi")
        setup_lo = sem("setup_lo")
        split_hi = sem("split_hi")
        split_lo = sem("split_lo")
        prod = sem("prod")
        prod_hi = sem("prod_hi")
        prod_lo = sem("prod_lo")
        prod_out = sem("prod_out")
        m_free = sem("m_free")
        m_store = sem("m_store")
        x_in = [sem(f"x_in{i}") for i in range(2)]
        q_ready = sem("q_ready")
        q_store = [sem(f"q_store{i}") for i in range(2)]
        q_free = sem("q_free")
        q_T = sem("q_T")
        q_Tout = sem("q_Tout")
        gate = sem("gate")
        gate_out = sem("gate_out")
        dve_chain = sem("dve_chain")
        exp_in = sem("exp_in")
        exp_out = sem("exp_out")
        hots_ready = sem("hots_ready")
        counted = sem("counted")
        slots_ready = sem("slots_ready")
        placed = sem("placed")
        routed = sem("routed")
        filled = sem("filled")
        ends_known = sem("ends_known")
        idx_ready = sem("idx_ready")
        idx_seen = sem("idx_seen")
        steps_ready = sem("steps_ready")
        ints_ready = sem("ints_ready")
        clipped = sem("clipped")
        scaled = sem("scaled")
        lower_done = sem("lower_done")
        first_done = sem("first_done")
        picked = sem("picked")
        pick_seen = sem("pick_seen")
        zero_hi = sem("zero_hi")
        zero_lo = sem("zero_lo")
        exp_hi = sem("exp_hi")
        exp_lo = sem("exp_lo")
        tin_in = [sem(f"tin_in{i}") for i in range(2)]
        t_T = sem("t_T")
        t_raw = sem("t_raw")
        t_lo = sem("t_lo")
        tile_done = sem("tile_done")
        y_out = sem("y_out")
        y_store = [sem(f"y_store{i}") for i in range(2)]
        m_hi = sem("m_hi")
        m_lo = sem("m_lo")
        m_in = [sem(f"m_in{i}") for i in range(2)]
        xc_in = [sem(f"xc_in{i}") for i in range(2)]
        ga_in = [sem(f"ga_in{i}") for i in range(2)]
        gb_in = [sem(f"gb_in{i}") for i in range(2)]
        x1_ready = sem("x1_ready")
        x1_kept = sem("x1_kept")
        x1_T = sem("x1_T")
        x1_hi = sem("x1_hi")
        x1_lo = sem("x1_lo")
        heads_ready = sem("heads_ready")
        b_store = sem("b_store")
        b_in = sem("b_in")
        low_done = sem("low_done")
        low_scaled = sem("low_scaled")
        low_hi = sem("low_hi")
        low_lo = sem("low_lo")
        layer_done = sem("layer_done")
        dense_out = sem("dense_out")
        scoresT = sem("scoresT")
        scT_out = sem("scT_out")
        scT_seen = sem("scT_seen")
        scores = sem("scores")
        nb_ready = sem("nb_ready")
        soft_done = sem("soft_done")
        cacc_ready = sem("cacc_ready")
        clu_done = sem("clu_done")
        csel_ready = sem("csel_ready")
        rowsel_done = sem("rowsel_done")
        out_ready = sem("out_ready")
        flag_ready = sem("flag_ready")
        again_in = [sem(f"again_in{i}") for i in range(2)]
        again_ready = sem("again_ready")
        again_seen = sem("again_seen")
        again_free = sem("again_free")
        again_store = [sem(f"again_store{i}") for i in range(2)]
        out_store = [sem(f"out_store{i}") for i in range(2)]

        N_CONST = 5
        STAGED = (16 * (1 + KC // 2), 16 * (1 + KC // 2), 0, 0)
        block = ctx.enter_context(nc.Block())

        def rows(i):
            return slice(i * P, (i + 1) * P) if isinstance(i, int) else bass.ds(i * P, P)

        def tile_of(tensor, t):
            return tensor[:, t, :] if isinstance(t, int) else tensor[:, bass.ds(t, 1), :].rearrange(
                "p o n -> p (o n)")

        def if_rows(engine, count, s, sure):
            return nullcontext() if sure else engine.If(count > s)

        PAIRS = ((0, FULL // 2 - 1, True), (FULL // 2 - 1, MT // 2, False))

        w1_v = w1.rearrange("(k p) (j i) -> j p k i", p=P, i=P)
        ew_v = expert_w.rearrange("e (k p) n -> (e k) p n", p=P)

        @block.sync
        def _(sp):
            sp.dma_start(stage[0:CL, 0, :], centroids).then_inc(stage_in[0], 16)
            for n, source in enumerate((thresholds, deltas, zero_points, scaling)):
                sp.dma_start(par[:, n, :], source.partition_broadcast(P)).then_inc(par_in, 16)
            sp.dma_start(xa[:, 0, :], x[rows(0), :]).then_inc(x_in[0], 16)
            sp.dma_start(stage[:, 1, :], lora_a.rearrange("a r i -> (a r) i")).then_inc(stage_in[1], 16)
            sp.dma_start(xa[:, 1, :], x[rows(1), :]).then_inc(x_in[1], 16)
            sp.dma_start(adp[:, :], adapter.partition_broadcast(P)).then_inc(const_in, 16)
            sp.dma_start(gw[:, :, :], gate_w.rearrange("(k p) e -> p k e", p=P)).then_inc(const_in, 16)
            with nc.allow_non_contiguous_dma(reason="a small column"):
                sp.dma_start(b1c[:, :], b1.rearrange("(k p) -> p k", p=P)).then_inc(const_in, 16)
            sp.dma_start(biasx[:, 0:H], b2.partition_broadcast(P)).then_inc(const_in, 16)
            sp.dma_start(gring[0:CL, 0, :].bitcast(I32),
                         assignments.partition_broadcast(CL)).then_inc(const_in, 16)
            with sp.Fori(0, KC // 2) as i:
                for b in range(2):
                    sp.wait_ge(setup_T, 2 * i + b + 1)
                    sp.dma_start(stage[:, b, :], w2[rows(2 * i + b), :]).then_inc(stage_in[b], 16)
            sp.wait_ge(setup_T, 2 + KC - 1)
            for k in range(KC):
                sp.dma_start(stage[:, 0, k * P:(k + 1) * P].rearrange("p (a r) -> p a r", a=A),
                             lora_b[:, k * P:(k + 1) * P, :].rearrange("a p r -> p a r")
                             ).then_inc(lora_in, 16)

            sp.dma_start(y_dram[FULL * P:, :], x[0:(MT - FULL) * P, :]).then_inc(filled, 16)

            def quantised(i, more):
                for b in range(2):
                    sp.wait_ge(q_ready, 2 * i + b + 2)
                    sp.dma_start(q_dram[rows(2 * i + b), :], qrow[:, b, :]).then_inc(q_store[b], 16)
                    if more:
                        sp.dma_start(xa[:, b, :], x[rows(2 * i + b + 2), :]).then_inc(x_in[b], 16)

            with sp.Fori(0, NT // 2 - 1) as i:
                quantised(i, True)
            quantised(NT // 2 - 1, False)

            def fetch(n, c):
                sp.dma_start(stage[:, c, :], ew_v[n] if isinstance(n, int) else
                             ew_v[bass.ds(n, 1)].rearrange("o p n -> p (o n)")).then_inc(stage_in[c], 16)

            sp.wait_ge(split_lo, KC + 2)
            for n in range(RING + KC):
                if n >= RING:
                    sp.wait_ge(zero_lo, n - RING + 1)
                fetch(n, n % RING)
            with sp.Fori(1 + KC // RING, E * KC // RING) as r:
                for c in range(RING):
                    sp.wait_ge(exp_lo, RING * r + c - RING - KC + 2)
                    fetch(RING * r + c, c)

            def load(t, b):
                sp.dma_start(stage[:, b, :], x[rows(t), :]).then_inc(xc_in[b], 16)

            def store(t, b):
                sp.wait_ge(out_ready, t + 1)
                sp.dma_start(out[rows(t), :], yout[:, b, :]).then_inc(out_store[b], 16)

            sp.wait_ge(exp_lo, (E - 1) * KC + 1)
            def adapter_rows(n):
                a = sp.value_load(adp[0:1, n:n + 1] if isinstance(n, int) else adp[0:1, bass.ds(n, 1)],
                                  min_val=0, max_val=A - 1)
                sp.dma_start(bwxf[LOW, :, :], b_dram[bass.ds(a * R, R), :, :]).then_inc(b_in, 16)

            for b in range(2):
                load(b, b)
            sp.wait_ge(b_store, 16)
            adapter_rows(0)
            sp.wait_ge(routed, 1)
            need = sp.value_load(freeat[0:1, E:E + 1], min_val=1, max_val=MT + 1)
            sp.wait_ge(tile_done, need)
            sp.wait_ge(m_store, 16 * KC)
            for k in range(KC):
                if k >= 2:
                    sp.wait_ge(m_in[k % 2], 16 * (k // 2))
                sp.dma_start(w2part(wf, 1)[:, k, :], m_dram[:, k, :]).then_inc(m_in[k % 2], 16)

            with sp.Fori(0, NT // 2 - 1) as i:
                for b in range(2):
                    sp.wait_ge(x1_ready, 2 * i + b + 3)
                    load(2 * i + b + 2, b)
                store(2 * i, 0)
                sp.wait_ge(layer_done, 2 * i + 2)
                adapter_rows(i + 1)
                store(2 * i + 1, 1)
            for b in range(2):
                store(NT - 2 + b, b)
            for b in range(2):
                sp.wait_ge(out_store[b], 16 * NT // 2)

            sp.wait_ge(flag_ready, 1)
            whole = sp.value_load(flag[0:1, 0:1], min_val=0, max_val=1)
            with sp.If(whole < 1):
                sp.sem_inc(again_free, 2)
                for b in range(2):
                    sp.dma_start(yout[:, b, :], out[rows(b), :]).then_inc(again_in[b], 16)

                def again(i, more):
                    for b in range(2):
                        sp.wait_ge(again_ready, 2 * i + b + 1)
                        sp.dma_start(out[rows(2 * i + b), :], tin[:, b, :]).then_inc(again_store[b], 16)
                        sp.wait_ge(again_store[b], 16 * i + 16)
                        sp.sem_inc(again_free, 1)
                        if more:
                            sp.dma_start(yout[:, b, :], out[rows(2 * i + b + 2), :]).then_inc(again_in[b], 16)

                with sp.Fori(0, NT // 2 - 1) as i:
                    again(i, True)
                again(NT // 2 - 1, False)
                for b in range(2):
                    sp.wait_ge(again_store[b], 16 * NT // 2)

        @block.gpsimd
        def _(pool):
            nc.gpsimd.memset(ident[:, :], 0.0).then_inc(iota_done, 1)
            pool.wait_ge(iota_done, 1)
            nc.gpsimd.affine_select(out=ident[:, :], in_=ident[:, :], compare_op=ALU.not_equal, fill=1.0,
                                    base=0, pattern=[[-1, P]], channel_multiplier=1).then_inc(iota_done, 1)
            kw = dict(allow_small_or_imprecise_dtypes=True)
            nc.gpsimd.iota(rowi[:, :], [[1, P]], base=0, channel_multiplier=0, **kw).then_inc(iota_done, 1)
            nc.gpsimd.iota(parti[:, :], [[0, 1]], base=0, channel_multiplier=1, **kw).then_inc(iota_done, 1)
            nc.gpsimd.iota(tcol[:, :, :], [[0, 2], [1, NT]], base=0, channel_multiplier=0,
                           **kw).then_inc(iota_done, 1)
            nc.gpsimd.iota(mt_row[:, :], [[1, MT]], base=0, channel_multiplier=0, **kw).then_inc(iota_done, 1)
            nc.gpsimd.iota(sc[:, 6, :], [[-1, E]], base=E, channel_multiplier=0, **kw).then_inc(iota_done, 1)
            nc.gpsimd.iota(sc[:, 5, :], [[1, A]], base=0, channel_multiplier=0, **kw).then_inc(iota_done, 1)

            pool.sem_inc(m_free, 2)
            pool.wait_ge(setup_T, 2 + KC)

            def load(j, b):
                pool.wait_ge(split_lo, j + 1)
                pool.dma_start(stage[:, 1 - b, :].rearrange("p (k i) -> p k i", k=KC),
                               w1_v[j]).then_inc(w1_in[1 - b], 16)

            def store(j):
                pool.wait_ge(prod_out, j + 2)
                pool.dma_start(m_dram[:, j, :], mev[:, j % 2, :]).then_inc(m_store, 16)
                pool.wait_ge(m_store, 16 * (j + 1))
                pool.sem_inc(m_free, 1)

            load(0, 0)
            for j in range(1, KC):
                load(j, j % 2)
                store(j - 1)
            store(KC - 1)

            for c in range(KC):
                pool.wait_ge(zero_hi, c + 1)
                nc.gpsimd.tensor_tensor(expart(wslots, 0, 1)[:, c, :], stage[:, c % RING, :],
                                        expart(wf, 0, 0)[:, c, :], ALU.subtract).then_inc(zero_lo, 1)

            pool.wait_ge(routed, 1)
            for b in range(2):
                pool.wait_ge(q_store[b], 16 * NT // 2)

            def gather(source, table, column, n, to, b, landed):
                copies[0] = copies[0] + 1
                nc.gpsimd.tensor_copy(idx[:, n, b:b + 1], table[:, column]).then_inc(idx_ready, 1)
                pool.wait_ge(idx_ready, copies[1] + copies[0])
                pool.sem_inc(idx_seen, 1)
                nc.gpsimd.indirect_dma_start(
                    out=to[:, b, :], out_offset=None, in_=source,
                    in_offset=bass.IndirectOffsetOnAxis(ap=idx[:, n, b:b + 1], axis=0)).then_inc(landed[b], 16)

            copies = [0, 0]
            for b in range(2):
                gather(q_dram, toku, slice(b, b + 1), 0, tin, b, tin_in)

            def rest(s, b):
                pool.wait_ge(t_raw, s + 1)
                nc.gpsimd.tensor_tensor(split[:, b, 1, :, :], gring[:, b, :].rearrange("p (k i) -> p k i", k=KC),
                                        splitf[:, b, 0, :, :], ALU.subtract).then_inc(t_lo, 1)

            count = pool.value_load(used[0:1, 0:1], min_val=FULL, max_val=MT)

            def turn(s, b, sure, sure_ahead, ahead=True):
                with if_rows(pool, count, s, sure):
                    rest(s, b)
                if ahead:
                    with if_rows(pool, count, s + 2, sure_ahead):
                        copies[:] = [0, s + 2]
                        pool.wait_ge(t_T, s + 1)
                        gather(q_dram, toku, bass.ds(s + 2, 1) if not isinstance(s, int) else
                               slice(s + 2, s + 3), 0, tin, b, tin_in)

            with pool.Fori(0, FULL // 2 - 1) as i:
                for b in range(2):
                    turn(2 * i + b, b, True, True)
            with pool.Fori(FULL // 2 - 1, MT // 2 - 1) as i:
                for b in range(2):
                    turn(2 * i + b, b, False, False)
            turn(MT - 3, 0, False, False)
            turn(MT - 2, 1, False, False, False)
            turn(MT - 1, 0, False, False, False)

            pool.wait_ge(ends_known, 1)
            all_of = [pool.value_load(stored[0:1, b:b + 1], min_val=8 * FULL, max_val=8 * MT + 8) for b in range(2)]
            for b in range(2):
                pool.wait_ge(y_store[b], all_of[b])
            pool.sem_inc(idx_seen, 1)
            copies[:] = [0, count]
            for b in range(2):
                for n, (to, landed) in enumerate(((gring, ga_in), (tin, gb_in))):
                    gather(y_dram, slotu[:, n, :], slice(b, b + 1), n, to, b, landed)
            with pool.Fori(1, NT // 2) as i:
                copies[:] = [4 * i, count]
                for b in range(2):
                    pool.wait_ge(x1_hi, 2 * i + b - 1)
                    for n, (to, landed) in enumerate(((gring, ga_in), (tin, gb_in))):
                        gather(y_dram, slotu[:, n, :], bass.ds(2 * i + b, 1), n, to, b, landed)

        @block.scalar
        def _(act):
            def setup_item(n, b, source_shape, to):
                act.wait_ge(setup_T, n + 1)
                nc.scalar.copy(to, source_shape).then_inc(setup_hi, 1)

            act.sem_inc(gate_out, 1)
            act.sem_inc(q_free, 2)
            act.sem_inc(prod_out, 1)
            act.wait_ge(steps_known, 1)

            def steps(t, b, landed, setup=None):
                act.wait_ge(x_in[b], landed)
                nc.scalar.activation(magnitude[:, b, :], xa[:, b, :], ACT.Abs)
                for g in range(G):
                    if g < G - 1:
                        act.wait_ge(picked, (G - 1) * t + g + 1)
                    else:
                        act.wait_ge(q_ready, t + 1)
                    nc.scalar.activation(bucket[g], xa[:, b, :], ACT.Identity, bias=rnd[:, 0:1],
                                         scale=by(par2[:, 1, :], g)).then_inc(steps_ready, 1)
                    if setup:
                        setup(g)

            def rounded(t):
                for g in range(OWN, G):
                    act.wait_ge(steps_ready, G * t + g + 1)
                    nc.scalar.activation(bucket[g], bucket[g], ACT.Identity, bias=rnd[:, 1:2]
                                         ).then_inc(ints_ready, 1)

            def dequantised(t):
                for g in range(OWN, G):
                    act.wait_ge(clipped, (G - OWN) * t + g - OWN + 1)
                    nc.scalar.activation(bucket[g], bucket[g], ACT.Copy, scale=by(par[:, 1, :], g)
                                         ).then_inc(scaled, 1)

            def take(t):
                act.wait_ge(q_T, t + 1)
                nc.scalar.copy(qT[:, :, :], pst[:, :, :]).then_inc(q_Tout, 1)

            def logits(t):
                act.wait_ge(gate, t + 1)
                nc.scalar.copy(rbuf[:, 0, bass.ds(t, 1), :],
                               psl[:, 0:E].unsqueeze(1)).then_inc(gate_out, 1)

            def release(b, stored):
                act.wait_ge(q_store[b], stored)
                act.sem_inc(q_free, 1)

            def weights(j, b):
                act.wait_ge(prod, j + 1)
                nc.scalar.copy(split[:, b, 0, :, :],
                               stage[:, 1 - b, :].rearrange("p (k i) -> p k i", k=KC)
                               ).then_inc(split_hi, 1)

            def merged(j, b):
                act.wait_ge(prod, j + 3)
                act.wait_ge(m_free, j + 1)
                nc.scalar.copy(mev[:, b, 0:H], main[:, b, :])
                nc.scalar.copy(mev[:, b, H:HX], psg[:, b * CL:(b + 1) * CL]).then_inc(prod_out, 1)

            def w2_item(g):
                setup_item(g + 2, g % 2, main[:, g % 2, :].rearrange("p (k c) -> p k c", k=KC),
                           w2part(wslots, 0)[:, :, g * P:(g + 1) * P])

            setup_item(0, 0, main[:, 0, 0:KC * CL].rearrange("p (k c) -> p k c", k=KC),
                       w2part(wslots, 0)[:, :, H:HX])
            setup_item(1, 1, main[:, 1, :].rearrange("p (k c) -> p k c", k=KC), ath[:, 0, :, :])
            steps(0, 0, 16, w2_item)
            rounded(0)
            dequantised(0)
            act.wait_ge(const_in, 16 * N_CONST)
            act.wait_ge(lora_in, 16 * KC)
            nc.scalar.copy(split[:, 0, 0, :, :], stage[:, 0, :].rearrange("p (k i) -> p k i", k=KC)
                           ).then_inc(split_hi, 1)
            nc.scalar.copy(split[:, 1, 0, :, :], b1c[:, :].unsqueeze(2).broadcast_to((P, KC, P))
                           ).then_inc(split_hi, 1)
            steps(1, 1, 16)
            rounded(1)
            dequantised(1)
            act.wait_ge(prod, 1)
            nc.scalar.copy(bwx[:, 0, 0:H], main[:, 0, :]).then_inc(prod_hi, 1)
            nc.scalar.copy(bwx[:, 0, H:HX], psg[:, 0:CL]).then_inc(prod_hi, 1)
            take(0)
            release(0, 16)

            def tile(t, c, landed, stored):
                steps(t, c, landed)
                logits(t - 2)
                rounded(t)
                dequantised(t)
                take(t - 1)
                release(1 - c, stored)

            with act.Fori(0, KC // 2 - 1) as i:
                for b in range(2):
                    j = 2 * i + b
                    act.wait_ge(w1_in[1 - b], 16 * i + 16)
                    weights(j, b)
                    tile(2 * j + 2, 0, 16 * j + 32, 16 * j + 16)
                    merged(j, b)
                    tile(2 * j + 3, 1, 16 * j + 32, 16 * j + 32)
            for b in range(2):
                j = KC - 2 + b
                act.wait_ge(w1_in[1 - b], 16 * (KC // 2))
                weights(j, b)
                tile(NT - 2 + b, b, 16 * NT // 2, 16 * (NT // 2 - 1 + b))
                merged(j, b)
            logits(NT - 2)
            take(NT - 1)
            logits(NT - 1)
            act.wait_ge(prod_lo, 1)
            act.dma_start(b_dram, bwxf).then_inc(b_store, 16)

            act.wait_ge(prod, KC + 2)
            for c in range(KC):
                act.wait_ge(stage_in[c % RING], STAGED[c % RING] + 16 * (c // RING + 1))
                nc.scalar.copy(expart(wslots, 0, 0)[:, c, :], stage[:, c % RING, :]).then_inc(zero_hi, 1)
            act.wait_ge(exp_in, 1)
            nc.scalar.activation(rcol[:, 3, :], rcol[:, 2, :], ACT.Exp).then_inc(exp_out, 1)

            def take(s, b):
                act.wait_ge(t_T, s + 1)
                if not (isinstance(s, int) and s == 0):
                    act.wait_ge(tile_done, s)
                nc.scalar.copy(split[:, b, 0, :, :], pst[:, :, :])
                nc.scalar.copy(gring[:, b, :].rearrange("p (k i) -> p k i", k=KC), pst[:, :, :]).then_inc(t_raw, 1)

            def give(i, s, b):
                act.wait_ge(tile_done, s + 2)
                if not (isinstance(i, int) and i == 0):
                    act.wait_ge(y_store[b], 16 * i)
                nc.scalar.copy(yout[:, b, :], main[:, b, :]).then_inc(y_out, 1)
                act.wait_ge(y_out, s + 3)
                act.dma_start(y_dram[rows(s), :], yout[:, b, :]).then_inc(y_store[b], 16)

            act.wait_ge(routed, 1)
            count = act.value_load(used[0:1, 0:1], min_val=FULL, max_val=MT)
            act.wait_ge(filled, 16)
            take(0, 0)

            def turn(i, sure):
                for b in range(2):
                    s = 2 * i + b
                    with if_rows(act, count, s + 1, sure):
                        take(s + 1, 1 - b)
                    with if_rows(act, count, s, sure):
                        give(i, s, b)

            turn(0, True)
            for first, end, sure in PAIRS:
                with act.Fori(max(first, 1), end) as i:
                    turn(i, sure)
            with if_rows(act, count, MT - 1, False):
                give(MT // 2, MT - 1, 0)

            def exps(i):
                for b in range(2):
                    act.wait_ge(nb_ready, i + 2)
                    nc.scalar.activation(el[:, b, :], zl[:, b, :], ACT.Exp, bias=smx[:, 1, b:b + 1],
                                         scale=1.0 / TEMPERATURE, accum_out=smx[:, 2, b:b + 1]
                                         ).then_inc(soft_done, 1)

            def high(t, b):
                act.wait_ge(x1_ready, t + 3)
                nc.scalar.copy(tile_of(x1, t), gring[:, b, :]).then_inc(x1_kept, 1)
                act.wait_ge(x1_T, t + 1)
                nc.scalar.copy(split[:, b, 0, :, :], pst[:, :, :]).then_inc(x1_hi, 1)

            def pair(i, more):
                act.wait_ge(low_scaled, i + 1)
                nc.scalar.copy(lowr[LOW, 0, :], lows).then_inc(low_hi, 1)
                if more:
                    adapter_columns(i + 1)
                if more:
                    high(2 * i + 2, 0)
                act.wait_ge(scoresT, i + 1)
                nc.scalar.copy(scT[0:CL, :], psg[0:CL, 0:2 * P]).then_inc(scT_out, 1)
                exps(i)
                if more:
                    high(2 * i + 3, 1)

            def adapter_columns(n):
                a = act.value_load(adp[0:1, n:n + 1] if isinstance(n, int) else adp[0:1, bass.ds(n, 1)],
                                   min_val=0, max_val=A - 1)
                nc.scalar.copy(heads_w[:, :, :, LOW], athf[:, :, :, bass.ds(a * R, R)]).then_inc(heads_ready, 1)

            for k in range(KC):
                act.wait_ge(m_in[k % 2], 16 * (k // 2 + 1))
                nc.scalar.copy(w2part(wslots, 0)[:, k, :], w2part(wf, 1)[:, k, :]).then_inc(m_hi, 1)
            adapter_columns(0)
            high(0, 0)
            act.wait_ge(m_lo, KC)
            for part in range(2):
                last = nc.scalar.copy(heads_w[:, part, :, 0:CL], w2part(wf, part)[:, :, H:HX])
            last.then_inc(heads_ready, 1)
            high(1, 1)
            with act.Fori(0, NT // 2 - 1) as i:
                pair(i, True)
            pair(NT // 2 - 1, False)

        @block.vector
        def _(dve):
            V = nc.vector
            chain = Chain(dve, dve_chain)
            dve.sem_inc(tile_done, 1)
            dve.sem_inc(y_out, 2)
            dve.sem_inc(exp_lo, 1)
            dve.sem_inc(x1_ready, 2)
            dve.sem_inc(dense_out, 2)
            dve.sem_inc(nb_ready, 1)
            dve.sem_inc(picked, G - 1)
            dve.sem_inc(q_ready, 1)
            dve.wait_ge(par_in, 64)
            dve.wait_ge(iota_done, 8)
            V.max(par2[:, 0, :], par[:, 0, :])
            V.reciprocal(par2[:, 1, :], par[:, 1, :])
            V.tensor_scalar(par2[:, 2, :], par[:, 2, :], -1.0, None, ALU.mult)
            V.tensor_scalar(par2[:, 3, :], par[:, 2, :], -1.0, LEVELS - 1.0, ALU.mult, ALU.add)
            V.memset(rnd[:, 0:1], ROUND)
            V.memset(rnd[:, 1:2], -ROUND).then_inc(steps_known, 1)

            def setup_item(n, source, hi, to):
                dve.wait_ge(setup_hi, n + 1)
                V.tensor_tensor(to, source, hi, ALU.subtract).then_inc(setup_lo, 1)

            def w2_item(g):
                at = slice(g * P, (g + 1) * P)
                setup_item(g + 2, main[:, g % 2, :].rearrange("p (k c) -> p k c", k=KC),
                           w2part(wf, 0)[:, :, at], w2part(wslots, 1)[:, :, at])

            def quantise(t, b, setup=lambda g: None):
                def low(g):
                    return by(par2[:, 2, :], g)

                def high(g):
                    return by(par2[:, 3, :], g)

                def above(g):
                    V.tensor_scalar(mask[:, g % 4, :], magnitude[:, b, :], by(par2[:, 0, :], g), None, ALU.is_gt)

                def pick(g):
                    dve.wait_ge(picked, (G - 1) * (t + 1) + g)
                    if g >= OWN:
                        dve.wait_ge(scaled, (G - OWN) * t + g - OWN + 1)
                    dve.sem_inc(pick_seen, 1)
                    V.copy_predicated(qrow[:, b, :], mask[:, g % 4, :], bucket[g]
                                      ).then_inc(picked if g < G - 1 else q_ready, 1)

                def finish(g):
                    return V.tensor_scalar(bucket[g], bucket[g], high(g), by(par[:, 1, :], g), ALU.min, ALU.mult)

                for g in range(OWN):
                    dve.wait_ge(steps_ready, G * t + g + 1)
                    last = V.tensor_scalar(bucket[g], bucket[g], ROUND, low(g), ALU.subtract, ALU.max)
                    if g == OWN - 1:
                        last.then_inc(lower_done, 1)
                    setup(g)
                above(1)
                dve.wait_ge(lower_done, t + 1)
                finish(0).then_inc(first_done, 1)
                for g in range(1, OWN):
                    finish(g)
                    setup(OWN + g - 1)
                dve.wait_ge(q_free, t + 1)
                dve.wait_ge(first_done, t + 1)
                V.scalar_tensor_tensor(qrow[:, b, :], magnitude[:, b, :], by(par2[:, 0, :], 0), bucket[0],
                                       ALU.is_gt, ALU.mult).then_inc(picked, 1)
                above(2)
                for g in range(1, OWN):
                    pick(g)
                    setup(2 * OWN + g - 2)
                    if g + 1 < OWN:
                        above(g + 2)
                for g in range(3 * OWN - 2, G):
                    setup(g)
                for g in range(OWN, G):
                    dve.wait_ge(ints_ready, (G - OWN) * t + g - OWN + 1)
                    V.tensor_scalar(bucket[g], bucket[g], low(g), high(g), ALU.max, ALU.min).then_inc(clipped, 1)
                    if g == OWN:
                        above(OWN + 1)
                for g in range(OWN, G):
                    pick(g)
                    if g + 2 < G:
                        above(g + 2)

            setup_item(0, main[:, 0, 0:KC * CL].rearrange("p (k c) -> p k c", k=KC),
                       w2part(wf, 0)[:, :, H:HX], w2part(wslots, 1)[:, :, H:HX])
            setup_item(1, main[:, 1, :].rearrange("p (k c) -> p k c", k=KC), athf[:, 0, :, :],
                       ath[:, 1, :, :])
            quantise(0, 0, w2_item)
            dve.wait_ge(split_hi, 1)
            V.tensor_tensor(split[:, 0, 1, :, :], stage[:, 0, :].rearrange("p (k i) -> p k i", k=KC),
                            splitf[:, 0, 0, :, :], ALU.subtract).then_inc(split_lo, 1)
            dve.wait_ge(split_hi, 2)
            V.tensor_tensor(split[:, 1, 1, :, :], b1c[:, :].unsqueeze(2).broadcast_to((P, KC, P)),
                            splitf[:, 1, 0, :, :], ALU.subtract).then_inc(split_lo, 1)
            V.memset(ones[:, :], 1.0)
            V.memset(freeat[:, 0:2], 1)
            V.tensor_scalar(tri[:, :], rowi[:, :], parti[:, :], None, ALU.is_gt)
            dve.wait_ge(const_in, 16 * N_CONST)
            chain(V.tensor_copy(gring[0:CL, 1, :], gring[0:CL, 0, :].bitcast(I32)))
            V.tensor_scalar(pickT[:, :], gring[0:CL, 1, :], parti[0:CL, :], None, ALU.is_equal)
            chain(V.tensor_copy(adpf[:, :], adp[:, :]))
            one = rbuf[:, 1, 0:E, :]
            chain(V.tensor_tensor(one, adpf[:, :].unsqueeze(2).broadcast_to((P, E, A)),
                                  sc[:, 5:6, :].broadcast_to((P, E, A)), ALU.is_equal))
            chain(V.tensor_tensor(one, one, par[:, 3:4, :].broadcast_to((P, E, A)), ALU.mult))
            V.tensor_reduce(comb[:, :], one, axis=AX.X, op=ALU.add).then_inc(consts, 1)
            quantise(1, 1)
            dve.wait_ge(prod_hi, 2)
            V.tensor_tensor(bwx[:, 1, 0:H], main[:, 0, :], bwxf[:, 0, 0:H], ALU.subtract)
            V.tensor_tensor(bwx[:, 1, H:HX], psg[:, 0:CL], bwxf[:, 0, H:HX], ALU.subtract).then_inc(prod_lo, 1)
            dve.wait_ge(prod, 2)
            V.tensor_tensor(biasx[:, 0:H], main[:, 1, :], biasx[:, 0:H], ALU.add)
            V.tensor_copy(biasx[:, H:HX], psl[:, 0:CL]).then_inc(prod_lo, 1)

            def weights(j, b):
                dve.wait_ge(split_hi, j + 3)
                V.tensor_tensor(split[:, b, 1, :, :], stage[:, 1 - b, :].rearrange("p (k i) -> p k i", k=KC),
                                splitf[:, b, 0, :, :], ALU.subtract).then_inc(split_lo, 1)

            with dve.Fori(0, KC // 2 - 1) as i:
                for b in range(2):
                    j = 2 * i + b
                    weights(j, b)
                    quantise(2 * j + 2, 0)
                    quantise(2 * j + 3, 1)
            for b in range(2):
                weights(KC - 2 + b, b)
                quantise(NT - 2 + b, b)

            dve.wait_ge(gate_out, NT + 1)

            def best(logits, hot, top):
                wide = rcol[:, top, :].unsqueeze(2).broadcast_to((P, NT, E))
                chain(V.tensor_reduce(rcol[:, top, :], logits, axis=AX.X, op=ALU.max))
                chain(V.tensor_tensor(rbuf[:, 1, :, :], logits, wide, ALU.is_equal))
                chain(V.tensor_tensor(rbuf[:, 1, :, :], rbuf[:, 1, :, :],
                                      sc[:, 6:7, :].broadcast_to((P, NT, E)), ALU.mult))
                chain(V.tensor_reduce(rcol[:, 4, :], rbuf[:, 1, :, :], axis=AX.X, op=ALU.max))
                chain(V.tensor_tensor(hot, rbuf[:, 1, :, :],
                                      rcol[:, 4, :].unsqueeze(2).broadcast_to((P, NT, E)), ALU.is_equal))

            best(rbuf[:, 0, :, :], rbuf[:, 2, :, :], 0)
            chain(V.scalar_tensor_tensor(rbuf[:, 4, :, :], rbuf[:, 2, :, :], -3.0e38, rbuf[:, 0, :, :],
                                         ALU.mult, ALU.add))
            best(rbuf[:, 4, :, :], rbuf[:, 3, :, :], 1)
            V.tensor_tensor(rcol[:, 2, :], rcol[:, 1, :], rcol[:, 0, :], ALU.subtract).then_inc(exp_in, 1)
            V.tensor_tensor(hotB[:, 0, :].rearrange("p (t e) -> p t e", e=E), rbuf[:, 2, :, :],
                            rbuf[:, 3, :, :], ALU.add).then_inc(hots_ready, 1)

            def scan(a, b, n, at):
                shift = 1
                while shift < n:
                    V.tensor_copy(at(b, 0, shift), at(a, 0, shift))
                    chain(V.tensor_tensor(at(b, shift, n), at(a, shift, n), at(a, 0, n - shift), ALU.add))
                    a, b, shift = b, a, 2 * shift
                return a

            dve.wait_ge(counted, 1)
            chain(V.tensor_copy(rbuf[:, 5, :, :], psg[:, 0:P].rearrange("p (t e) -> p t e", e=E)))
            chain(V.tensor_copy(rbuf[:, 6, :, :], rbuf[:, 5, :, :]))
            s = scan(6, 7, NT, lambda buf, lo, hi: rbuf[:, buf, lo:hi, :])
            chain(V.tensor_tensor(rbuf[:, 8, :, :], rbuf[:, s, :, :], rbuf[:, 5, :, :], ALU.subtract))
            chain(V.tensor_tensor(rbuf[:, 8, :, :], rbuf[:, 8, :, :],
                                  psl[:, 0:P].rearrange("p (t e) -> p t e", e=E), ALU.add))
            chain(V.tensor_scalar(tint[:, :], rbuf[:, s, NT - 1, :], P - 1.0, None, ALU.add))
            chain(V.tensor_scalar(tint[:, :], tint[:, :], 7, None, ALU.logical_shift_right))
            chain(V.tensor_copy(sc[:, 0, :], tint[:, :]))
            chain(V.tensor_copy(sc[:, 1, :], sc[:, 0, :]))
            s = scan(1, 2, E, lambda buf, lo, hi: sc[:, buf, lo:hi])
            ends = sc[:, s, :]
            chain(V.tensor_tensor(sc[:, 3, :], ends, sc[:, 0, :], ALU.subtract))
            chain(V.scalar_tensor_tensor(rbuf[:, 9, :, :], sc[:, 3:4, :].broadcast_to((P, NT, E)), float(P),
                                         rbuf[:, 8, :, :], ALU.mult, ALU.add))
            for n in range(2):
                chain(V.tensor_tensor(rbuf[:, 4 + n, :, :], rbuf[:, 9, :, :], rbuf[:, 2 + n, :, :], ALU.mult))
                chain(V.tensor_reduce(slots[:, n, :], rbuf[:, 4 + n, :, :], axis=AX.X, op=ALU.add))
            V.tensor_copy(slotu[:, :, :], slots[:, :, :])
            chain(V.tensor_copy(sli[:, :, :], slots[:, :, :]))
            chain(V.tensor_scalar(sli2[:, 0, :, :], sli[:, :, :], 7, None, ALU.logical_shift_right))
            chain(V.tensor_scalar(sli2[:, 1, :, :], sli[:, :, :], P - 1, None, ALU.bitwise_and))
            V.tensor_copy(shi[:, :, :], sli2[:, 0, :, :])
            chain(V.tensor_copy(slo[:, :, :], sli2[:, 1, :, :]))
            n2 = 2 * NT
            flat = lambda a: a.rearrange("p n t -> p (n t)")
            V.tensor_tensor(hotB[:, :, :], rowi[:, :].unsqueeze(1).broadcast_to((P, n2, P)),
                            flat(slo[:, :, :]).unsqueeze(2).broadcast_to((P, n2, P)), ALU.is_equal)
            chain(V.tensor_tensor(hotA[:, :, :], mt_row[:, :].unsqueeze(1).broadcast_to((P, n2, MT)),
                                  flat(shi[:, :, :]).unsqueeze(2).broadcast_to((P, n2, MT)), ALU.is_equal))
            V.tensor_scalar(hotX[:, :, 0:MT], hotA[:, :, :], parti[:, :], None, ALU.mult)
            V.tensor_tensor(hotX[:, :, MT:2 * MT], hotA[:, :, :],
                            flat(tcol[:, :, :]).unsqueeze(2).broadcast_to((P, n2, MT)),
                            ALU.mult).then_inc(slots_ready, 1)
            chain(V.tensor_tensor(mt_cmp[:, :, :], mt_row[:, :].unsqueeze(2).broadcast_to((P, MT, E - 1)),
                                  ends[:, 0:E - 1].unsqueeze(1).broadcast_to((P, MT, E - 1)), ALU.is_ge))
            chain(V.tensor_reduce(mt_exp[:, :], mt_cmp[:, :, :], axis=AX.X, op=ALU.add))
            V.tensor_scalar(mt_need[:, :], mt_exp[:, :], float(KC), 1.0, ALU.mult, ALU.add)
            V.tensor_copy(used[:, :], ends[:, E - 1:E])
            V.tensor_scalar(freeat[:, 2:E + 1], ends[:, 0:E - 1], 1.0, None, ALU.add)
            chain(V.tensor_copy(mt_int[:, :], mt_exp[:, :]))
            chain(V.tensor_scalar(mt_int[:, :], mt_int[:, :], 1, None, ALU.bitwise_and))
            chain(V.tensor_copy(mt_exp[:, :], mt_int[:, :]))
            chain(V.tensor_scalar(mt_par[:, :], mt_exp[:, :], float(SLOT1), None, ALU.mult))
            dve.wait_ge(placed, 1)
            chain(V.tensor_copy(mt_cmp[:, :, 0], psg[:, 0:MT]))
            V.scalar_tensor_tensor(toku[:, :], psg[:, MT:2 * MT], float(P), mt_cmp[:, :, 0], ALU.mult,
                                   ALU.add).then_inc(routed, 1)
            V.tensor_scalar(stored[:, 0:1], used[:, :], 1.0, None, ALU.add)
            chain(V.tensor_copy(stored[:, 1:2], used[:, :]))
            V.tensor_scalar(stored[:, :], stored[:, :], 1, 4, ALU.logical_shift_right,
                            ALU.logical_shift_left).then_inc(ends_known, 1)
            dve.wait_ge(exp_out, 1)
            chain(V.tensor_scalar(rcol[:, 5, :], rcol[:, 3, :], 1.0, None, ALU.add))
            chain(V.reciprocal(wts[:, 0, :], rcol[:, 5, :]))
            V.tensor_tensor(wts[:, 1, :], rcol[:, 3, :], wts[:, 0, :], ALU.mult)

            def expert(e, odd):
                for c in range(KC):
                    dve.wait_ge(stage_in[c % RING], STAGED[c % RING] + 16 * (c // RING + 1) + e * 32)
                    V.tensor_copy(expart(wslots, odd, 0)[:, c, :], stage[:, c % RING, :]).then_inc(exp_hi, 1)
                    dve.wait_ge(exp_hi, (e - 1) * KC + c + 1)
                    V.tensor_tensor(expart(wslots, odd, 1)[:, c, :], stage[:, c % RING, :],
                                    expart(wf, odd, 0)[:, c, :], ALU.subtract).then_inc(exp_lo, 1)

            dve.wait_ge(m_store, 16 * KC)
            for b in range(2):
                dve.wait_ge(q_store[b], 16 * NT // 2)
            expert(1, 1)
            with dve.Fori(1, E // 2) as pair:
                for odd in range(2):
                    need = dve.value_load(freeat[0:1, bass.ds(2 * pair + odd, 1)], min_val=1, max_val=MT + 1)
                    dve.wait_ge(tile_done, need)
                    expert(2 * pair + odd, odd)

            def merged(k):
                dve.wait_ge(m_hi, k + 1)
                V.tensor_tensor(w2part(wslots, 1)[:, k, :], w2part(wf, 1)[:, k, :], w2part(wf, 0)[:, k, :],
                                ALU.subtract).then_inc(m_lo, 1)

            for k in range(KC // 2 + 2):
                merged(k)

            dve.wait_ge(ends_known, 1)
            all_of = [dve.value_load(stored[0:1, b:b + 1], min_val=8 * FULL, max_val=8 * MT + 8) for b in range(2)]
            for b in range(2):
                dve.wait_ge(y_store[b], all_of[b])
            dve.sem_inc(pick_seen, 1)

            def total(i, b, t):
                dve.wait_ge(xc_in[b], 16 * i + 16)
                dve.wait_ge(ga_in[b], 16 * i + 16)
                dve.wait_ge(gb_in[b], 16 * i + 16)
                at = (lambda n: wts[:, n, t:t + 1]) if isinstance(t, int) else (
                    lambda n: wts[:, n, bass.ds(t, 1)])
                chain(V.scalar_tensor_tensor(gring[:, b, :], gring[:, b, :], at(0), stage[:, b, :],
                                             ALU.mult, ALU.add))
                V.scalar_tensor_tensor(gring[:, b, :], tin[:, b, :], at(1), gring[:, b, :],
                                       ALU.mult, ALU.add).then_inc(x1_ready, 1)

            def low(t, b):
                dve.wait_ge(x1_hi, t + 1)
                V.tensor_tensor(split[:, b, 1, :, :], pst[:, :, :], splitf[:, b, 0, :, :],
                                ALU.subtract).then_inc(x1_lo, 1)

            def scale(i):
                dve.wait_ge(low_done, i + 1)
                V.tensor_scalar(lows, psg[LOW, 0:2 * P], comb[LOW, bass.ds(i, 1)], None,
                                ALU.mult).then_inc(low_scaled, 1)
                dve.wait_ge(low_hi, i + 1)
                V.tensor_tensor(lowr[LOW, 1, :], lows, lowrf[LOW, 0, :], ALU.subtract).then_inc(low_lo, 1)

            def result(i, t, b):
                if not (isinstance(i, int) and i == 0):
                    dve.wait_ge(out_store[b], 16 * i)
                dve.wait_ge(layer_done, t + 1)
                V.tensor_tensor(yout[:, b, :], main[:, b, :], biasx[:, 0:H], ALU.add).then_inc(dense_out, 1)

            def add(t, b):
                dve.wait_ge(x1_kept, t + 1)
                dve.wait_ge(dense_out, t + 3)
                V.scalar_tensor_tensor(yout[:, b, :], yout[:, b, :], qsel[:, bass.ds(t, 1)],
                                       tile_of(x1, t), ALU.mult, ALU.add).then_inc(out_ready, 1)

            def judge(i):
                dve.wait_ge(scores, i + 1)
                chain(V.tensor_tensor(zl[:, :, :], psl[:, 0:2 * CL].rearrange("p (b c) -> p b c", b=2),
                                      biasx[:, H:HX].unsqueeze(1).broadcast_to((P, 2, CL)), ALU.add))
                chain(V.tensor_reduce(smx[:, 0, :], zl[:, :, :], axis=AX.X, op=ALU.max))
                V.tensor_scalar(smx[:, 1, :], smx[:, 0, :], -1.0 / TEMPERATURE, None, ALU.mult).then_inc(nb_ready, 1)
                dve.wait_ge(soft_done, 2 * i + 2)
                chain(V.reciprocal(smx[:, 3, :], smx[:, 2, :]))
                for b in range(2):
                    last = V.tensor_scalar(hits[:, b, :], el[:, b, :], smx[:, 3, b:b + 1], THRESHOLD,
                                           ALU.mult, ALU.is_gt)
                chain(last)
                V.tensor_reduce(qsel[:, bass.ds(2 * i, 2)], hits[:, :, :], axis=AX.X, op=ALU.max)
                for b in range(2):
                    chain(V.tensor_tensor(cacc[:, :], cacc[:, :], hits[:, b, :], ALU.max))

            def whole(i, more):
                if more:
                    total(i + 1, 0, 2 * i + 2)
                scale(i)
                if more:
                    low(2 * i + 2, 0)
                    total(i + 1, 1, 2 * i + 3)
                result(i, 2 * i, 0)
                judge(i)
                if not more:
                    V.tensor_copy(caccb[:, :], cacc[:, :]).then_inc(cacc_ready, 1)
                add(2 * i, 0)
                result(i, 2 * i + 1, 1)
                add(2 * i + 1, 1)
                if more:
                    low(2 * i + 3, 1)

            V.memset(cacc[:, :], 0.0)
            total(0, 0, 0)
            for k in range(KC // 2 + 2, KC):
                merged(k)
            total(0, 1, 1)
            low(0, 0)
            low(1, 1)
            chain.turn(0, chain.here(), 0)
            whole(0, True)
            first, per = chain.here(), 8
            with dve.Fori(1, NT // 2 - 1) as i:
                chain.turn(i - 1, first, per)
                whole(i, True)
                assert chain.n == per, chain.n
            chain.turn(0, first + per * (NT // 2 - 2), 0)
            whole(NT // 2 - 1, False)

            dve.wait_ge(clu_done, 1)
            chain(V.tensor_copy(clu[:, :], psl[0:CL, 0:1]))
            V.tensor_scalar(cselb[:, :], ones[0:CL, :], clu[:, :], 0.5, ALU.mult, ALU.is_gt
                            ).then_inc(csel_ready, 1)
            dve.wait_ge(rowsel_done, 1)
            chain(V.tensor_reduce(smx[:, 0, 0:1], main[:, 0, :], axis=AX.X, op=ALU.min))
            V.tensor_copy(flag[:, :], smx[:, 0, 0:1]).then_inc(flag_ready, 1)
            dve.wait_ge(flag_ready, 1)
            full = dve.value_load(flag[0:1, 0:1], min_val=0, max_val=1)
            with dve.If(full < 1):
                count = gring[:, 0, :].bitcast(U8)[:, 0:H]
                V.tensor_scalar(count, main[:, 0, :], 0.5, None, ALU.is_gt).then_inc(again_seen, 1)
                dve.wait_ge(again_seen, 1)
                with dve.Fori(0, NT // 2) as i:
                    for b in range(2):
                        dve.wait_ge(again_in[b], 16 * i + 16)
                        dve.wait_ge(again_free, 2 * i + b + 1)
                        V.tensor_copy(tin[:, b, :], tile_of(x1, 2 * i + b)).then_inc(again_seen, 1)
                        dve.wait_ge(again_seen, 4 * i + 2 * b + 2)
                        dve.sem_inc(again_seen, 1)
                        V.copy_predicated(tin[:, b, :], count, yout[:, b, :]).then_inc(again_ready, 1)

        @block.tensor
        def _(pe):
            def mm(o, l, r, start, stop):
                return nc.tensor.matmul(o, l, r, start=start, stop=stop)

            def three(cols, stationary, moving):
                for k in range(KC):
                    for sp_, mp in ((0, 0), (0, 1), (1, 0)):
                        for o, lo, hi in cols:
                            last = mm(o, stationary(k, sp_), moving(k, mp, lo, hi),
                                      k == 0 and (sp_, mp) == (0, 0), k == KC - 1 and (sp_, mp) == (1, 0))
                return last

            pe.wait_ge(iota_done, 2)
            pe.wait_ge(stage_in[0], 16)
            for k in range(KC):
                last = nc.tensor.transpose(main[:, 0, k * CL:(k + 1) * CL], stage[0:CL, 0, k * P:(k + 1) * P],
                                           ident[0:CL, 0:CL])
            last.then_inc(setup_T, 1)
            pe.wait_ge(stage_in[1], 16)
            for k in range(KC):
                last = nc.tensor.transpose(main[:, 1, k * P:(k + 1) * P], stage[:, 1, k * P:(k + 1) * P],
                                           ident[:, :])
            last.then_inc(setup_T, 1)
            with pe.Fori(0, KC // 2) as i:
                for b in range(2):
                    pe.wait_ge(stage_in[b], 16 * i + 32)
                    pe.wait_ge(setup_lo, 2 * i + b + 1)
                    for k in range(KC):
                        last = nc.tensor.transpose(main[:, b, k * P:(k + 1) * P],
                                                   stage[:, b, k * P:(k + 1) * P], ident[:, :])
                    last.then_inc(setup_T, 1)
            pe.wait_ge(setup_lo, KC + 2)

            def product(m, b, scores_to=None):
                pe.wait_ge(split_lo, m + 1)
                last = three([(main[:, b, 0:NB], 0, NB), (main[:, b, NB:H], NB, H),
                              (psg[:, b * CL:(b + 1) * CL] if scores_to is None else scores_to, H, HX)],
                             lambda k, part: split[:, b, part, k, :],
                             lambda k, part, lo, hi: w2part(wslots, part)[:, k, lo:hi])
                last.then_inc(prod, 1)

            def turn_q(t, b):
                pe.wait_ge(q_ready, t + 2)
                for k in range(KC):
                    last = nc.tensor.transpose(pst[:, k, :], qrow[:, b, k * P:(k + 1) * P], ident[:, :])
                last.then_inc(q_T, 1)

            def gating(t):
                pe.wait_ge(q_Tout, t + 1)
                pe.wait_ge(gate_out, t + 1)
                for k in range(KC):
                    last = mm(psl[:, 0:E], qT[:, k, :], gw[:, k, :], k == 0, k == KC - 1)
                last.then_inc(gate, 1)

            product(0, 0)
            turn_q(0, 0)
            product(1, 1, psl[:, 0:CL])
            pe.wait_ge(consts, 1)
            pe.wait_ge(prod_lo, 2)
            gating(0)

            def block_of_w1(j, b, t):
                turn_q(t - 1, 1 - t % 2 if isinstance(t, int) else 1)
                pe.wait_ge(prod_out, j + 1)
                product(j + 2, b)
                gating(t - 1)

            with pe.Fori(0, KC // 2 - 1) as i:
                for b in range(2):
                    j = 2 * i + b
                    block_of_w1(j, b, 2 * j + 2)
                    turn_q(2 * j + 2, 0)
                    gating(2 * j + 2)
            block_of_w1(KC - 2, 0, NT - 2)
            block_of_w1(KC - 1, 1, NT - 1)
            turn_q(NT - 1, 1)
            gating(NT - 1)

            pe.wait_ge(prod_out, KC + 1)
            pe.wait_ge(gate_out, NT + 1)
            pe.wait_ge(hots_ready, 1)
            mm(psl[:, 0:P], tri[:, :], hotB[:, 0, :], True, True)
            mm(psg[:, 0:P], ones[:, :], hotB[:, 0, :], True, True).then_inc(counted, 1)
            pe.wait_ge(slots_ready, 1)
            for n in range(2 * NT):
                last = mm(psg[:, 0:2 * MT], hotB[:, n, :], hotX[:, n, :], n == 0, n == 2 * NT - 1)
            last.then_inc(placed, 1)
            pe.wait_ge(routed, 1)

            def turn_rows(nth, s, b):
                pe.wait_ge(tin_in[b], 16 * nth)
                for k in range(KC):
                    last = nc.tensor.transpose(pst[:, k, :], tin[:, b, k * P:(k + 1) * P], ident[:, :])
                last.then_inc(t_T, 1)

            count = pe.value_load(used[0:1, 0:1], min_val=FULL, max_val=MT)

            def multiply(s, b, nth, sure, ahead=True):
                with if_rows(pe, count, s, sure):
                    pe.wait_ge(t_lo, s + 1)
                if ahead:
                    with if_rows(pe, count, s + 1, sure):
                        turn_rows(nth, s + 1, 1 - b)
                at = (lambda tab: tab[0:1, s:s + 1]) if isinstance(s, int) else (
                    lambda tab: tab[0:1, bass.ds(s, 1)])
                need = pe.value_load(at(mt_need), min_val=1, max_val=E * KC)
                base = pe.value_load(at(mt_par), min_val=0, max_val=SLOT1)
                with if_rows(pe, count, s, sure):
                    pe.wait_ge(exp_lo, need)
                    pe.wait_ge(y_out, s + 1)
                    for k in range(KC):
                        for sp_, mp in ((0, 0), (0, 1), (1, 0)):
                            for h in range(2):
                                last = mm(main[:, b, h * NB:(h + 1) * NB], split[:, b, sp_, k, :],
                                          wslots[:, bass.ds(base + mp * WE + k * H + h * NB, NB)],
                                          k == 0 and (sp_, mp) == (0, 0), k == KC - 1 and (sp_, mp) == (1, 0))
                    last.then_inc(tile_done, 1)

            turn_rows(1, 0, 0)
            pe.wait_ge(zero_lo, KC)
            for first, end, sure in PAIRS:
                with pe.Fori(first, end) as i:
                    multiply(2 * i, 0, i + 1, sure)
                    multiply(2 * i + 1, 1, i + 2, sure)
            multiply(MT - 1, 0, 0, False, ahead=False)

            def turn_x1(t, b):
                pe.wait_ge(x1_ready, t + 3)
                for k in range(KC):
                    last = nc.tensor.transpose(pst[:, k, :], gring[:, b, k * P:(k + 1) * P], ident[:, :])
                last.then_inc(x1_T, 1)

            def heads(b):
                return [(main[:, b, 0:NB], 0, NB), (main[:, b, NB:H], NB, H)]

            def product1(t, b, first=0, end=KC):
                if first == 0:
                    pe.wait_ge(dense_out, t + 1)
                    pe.wait_ge(x1_lo, t + 1)
                for k in range(first, end):
                    for sp_, mp in ((0, 0), (0, 1), (1, 0)):
                        for o, lo, hi in heads(b):
                            mm(o, split[:, b, sp_, k, :], w2part(wslots, mp)[:, k, lo:hi],
                               k == 0 and (sp_, mp) == (0, 0), False)

            def lora(b):
                for sp_, mp in ((0, 0), (0, 1), (1, 0)):
                    for o, lo, hi in heads(b):
                        last = mm(o, lowr[LOW, sp_, b * P:(b + 1) * P], bwx[LOW, mp, lo:hi], False,
                                  (sp_, mp) == (1, 0))
                last.then_inc(layer_done, 1)

            def both(part, k):
                return split[:, :, part, k, :]

            def pair(i, more):
                product1(2 * i, 0)
                pe.wait_ge(x1_lo, 2 * i + 2)
                pe.wait_ge(nb_ready, i + 1)
                pe.wait_ge(heads_ready, i + 2)
                last = three([(psg[0:CL + R, 0:2 * P], 0, 0)], lambda k, part: heads_w[:, part, k, :],
                             lambda k, part, lo, hi: both(part, k))
                last.then_inc(low_done, 1)
                if more:
                    turn_x1(2 * i + 2, 0)
                product1(2 * i + 1, 1, 0, 2)
                pe.wait_ge(low_lo, i + 1)
                pe.wait_ge(b_in, 16 * i + 16)
                for sp_, mp in ((0, 0), (0, 1), (1, 0)):
                    last = nc.tensor.matmul(psg[0:CL, 0:2 * P], bwx[LOW, sp_, H:HX], lowr[LOW, mp, :],
                                            start=False, stop=(sp_, mp) == (1, 0), skip_group_check=True)
                last.then_inc(scoresT, 1)
                lora(0)
                product1(2 * i + 1, 1, 2, 3)
                pe.wait_ge(scT_out, i + 1)
                pe.sem_inc(scT_seen, 1)
                for b in range(2):
                    last = nc.tensor.transpose(psl[:, b * CL:(b + 1) * CL], scT[0:CL, b * P:(b + 1) * P],
                                               ident[0:CL, 0:CL])
                last.then_inc(scores, 1)
                product1(2 * i + 1, 1, 3)
                lora(1)
                if more:
                    turn_x1(2 * i + 3, 1)

            turn_x1(0, 0)
            pe.wait_ge(x1_lo, 1)
            turn_x1(1, 1)
            pe.wait_ge(m_lo, KC)
            with pe.Fori(0, NT // 2 - 1) as i:
                pair(i, True)
            pair(NT // 2 - 1, False)

            pe.wait_ge(cacc_ready, 1)
            mm(psl[0:CL, 0:1], caccb[:, :], ones[:, 0:1], True, True).then_inc(clu_done, 1)
            pe.wait_ge(csel_ready, 1)
            mm(main[:, 0, 0:NB], cselb[:, :], pickT[:, 0:NB], True, True)
            mm(main[:, 0, NB:H], cselb[:, :], pickT[:, NB:H], True, True).then_inc(rowsel_done, 1)


_INS = ["x", "condB_thresholds", "condB_deltas", "condB_zeropoints", "itok_B_1_7", "L0_ffn_gate_w",
        "L0_ffn_expert_w", "L1_cond_weight", "L1_cond_bias", "L1_cond_lora_a_weights",
        "L1_cond_lora_b_weights", "L1_cond_scaling_factors", "L1_ffn_weight", "L1_ffn_bias",
        "L1_ffn_centroids", "L1_ffn_assignments"]


def kernel(**inputs):
    import concourse.bacc as bacc
    from concourse.bass_utils import run_bass_kernel_spmd

    nc = bacc.Bacc("TRN2", target_bir_lowering=False, num_devices=1, dynamic_dma_scratch_size=4096)
    arrays, args = {}, []
    for name in _INS:
        a = np.ascontiguousarray(inputs[name])
        if name == "x":
            a = a.reshape(TOK, H)
        arrays[f"in_{name}"] = a
        args.append(nc.dram_tensor(f"in_{name}", a.shape, mybir.dt.from_np(a.dtype), kind="ExternalInput").ap())
    out = nc.dram_tensor("out", [TOK, H], F32, kind="ExternalOutput").ap()
    build(nc, *args, out)
    r = run_bass_kernel_spmd(nc, [arrays], core_ids=[0])
    return r.results[0]["out"].reshape(inputs["x"].shape)
```
